# Optimizing a Trainium2 kernel written in Bass

```python
import numpy as np
import jax
import jax.numpy as jnp

def _softmax(x, axis=-1):
    return jax.nn.softmax(x, axis=axis)

def _gelu(x):
    return jax.nn.gelu(x, approximate=True)

def _silu(x):
    return jax.nn.silu(x)

def _sigmoid(x):
    return jax.nn.sigmoid(x)

def _layernorm(x, axis=-1, eps=1e-05):
    m = jnp.mean(x, axis=axis, keepdims=True)
    v = jnp.var(x, axis=axis, keepdims=True)
    return (x - m) / jnp.sqrt(v + eps)

def _scatter_add(tgt, idx, src, axis=0):
    return tgt.at[idx].add(src)

def _segment_sum(src, seg, n):
    return jax.ops.segment_sum(src, seg, n)
kernel_name = 'mk_flamingo_gated_d4_seqx_r8_870fe3'

def setup_inputs(seed: int=0):
    np.random.seed(seed)
    _w = jnp.asarray

    def _rec_inputs():
        import jax
        import jax.numpy as jnp
        _rk = jax.random.key(seed)
        x = 7.22e-05 + 1 * jax.random.normal(jax.random.fold_in(_rk, 1), (64, 128, 128), jnp.float32)
        _lenS = 128 - jax.random.randint(jax.random.fold_in(_rk, 7), (64,), 0, max(1, 128 // 4) + 1, jnp.int32)
        _lenS2 = 120 - jax.random.randint(jax.random.fold_in(_rk, 8), (64,), 0, max(1, 120 // 4) + 1, jnp.int32)
        _ctx_1024P = jax.random.normal(jax.random.fold_in(_rk, 11), (64, 16, 128), jnp.float32)
        _ctx_1024c = jax.random.dirichlet(jax.random.fold_in(_rk, 511), 0.3 * jnp.ones((16,), jnp.float32), (64, 120))
        _ctx_1024t = jnp.einsum('bsk,bkd->bsd', _ctx_1024c, _ctx_1024P)
        _ctx_1024t = _ctx_1024t * jax.lax.rsqrt(jnp.mean(jnp.square(_ctx_1024t)) + 1e-12) * 0.953939
        ctx_1024 = 4.13588e-05 + 0.999923 * (_ctx_1024t + 0.3 * jax.random.normal(jax.random.fold_in(_rk, 611), (64, 120, 128), jnp.float32))
        _validS = jnp.arange(128)[None, :] < _lenS[:, None]
        _validS2 = jnp.arange(120)[None, :] < _lenS2[:, None]
        _causal = jnp.tril(jnp.ones((128, 128), dtype=bool))
        mask_1x1xSxS2_ik1 = jnp.where(jnp.broadcast_to(_validS2[0:1, None, None, :], (1, 1, 128, 120)), 1, 0).astype(jnp.int32)
        _g = jax.random.normal(jax.random.fold_in(_rk, 9001), (2, 4), jnp.float32)
        _g = jnp.sign(_g) * jnp.maximum(jnp.abs(_g), 1.0) + (_g == 0) * 1.0
        g_xattn = _g[0]
        g_ffn = _g[1]
        return (x, ctx_1024, mask_1x1xSxS2_ik1, g_xattn, g_ffn)
    x, ctx_1024, mask_1x1xSxS2_ik1, g_xattn, g_ffn = _rec_inputs()

    def _L0_xattn_setup():
        import jax, jax.numpy as jnp
        import numpy as np
        EMBED = 128
        HEADS = 16
        HEAD_DIM = EMBED // HEADS
        B, S = (4, 256)
        key = jax.random.key(seed)
        ks = jax.random.split(key, 9)
        q = jax.random.normal(ks[0], (B, S, EMBED), dtype=jnp.float32)
        k = jax.random.normal(ks[1], (B, S, EMBED), dtype=jnp.float32)
        v = jax.random.normal(ks[2], (B, S, EMBED), dtype=jnp.float32)
        mask = jax.random.randint(ks[3], (1, 1, S, S), 0, 2, dtype=jnp.int32)
        sc = 1.0 / np.sqrt(HEAD_DIM)
        Wq = jax.random.normal(ks[4], (HEAD_DIM, HEAD_DIM), dtype=jnp.float32) * sc
        Wk = jax.random.normal(ks[5], (HEAD_DIM, HEAD_DIM), dtype=jnp.float32) * sc
        Wv = jax.random.normal(ks[6], (HEAD_DIM, HEAD_DIM), dtype=jnp.float32) * sc
        Wo = jax.random.normal(ks[7], (EMBED, EMBED), dtype=jnp.float32) * (1.0 / np.sqrt(EMBED))
        bo = jax.random.normal(ks[8], (EMBED,), dtype=jnp.float32) * 0.01
        return {'q': q, 'k': k, 'v': v, 'mask': mask, 'Wq': Wq, 'Wk': Wk, 'Wv': Wv, 'Wo': Wo, 'bo': bo}
    _L0_xattn_all = _L0_xattn_setup()
    _L0_xattn_in = {k: v for k, v in _L0_xattn_all.items() if k in ('Wq', 'Wk', 'Wv', 'Wo', 'bo')}
    del _L0_xattn_all

    def _L0_ffn_setup():
        import jax, jax.numpy as jnp
        import numpy as np
        H = 16
        TOP_K = 2
        LN_EPS = 1e-05
        key = jax.random.key(seed)
        ks = jax.random.split(key, 8)
        B, S, E, NE = (2, 128, 128, 8)
        w = lambda k, shp: jax.random.normal(k, shp, dtype=jnp.float32) * 0.02
        return {'x': jax.random.normal(ks[0], (B, S, E), dtype=jnp.float32), 'rW1': w(ks[1], (E // 2, E)), 'rb1': jnp.zeros((E // 2,), jnp.float32), 'ln_g': jnp.ones((E // 2,), jnp.float32), 'ln_b': jnp.zeros((E // 2,), jnp.float32), 'rW2': w(ks[2], (NE, E // 2)), 'rb2': jnp.zeros((NE,), jnp.float32), 'qW': w(ks[3], (NE, E, E)), 'qb': jnp.zeros((NE, E), jnp.float32), 'kW': w(ks[4], (NE, E, E)), 'kb': jnp.zeros((NE, E), jnp.float32), 'vW': w(ks[5], (NE, E, E)), 'vb': jnp.zeros((NE, E), jnp.float32), 'oW': w(ks[6], (NE, E, E)), 'ob': jnp.zeros((NE, E), jnp.float32)}
    _L0_ffn_all = _L0_ffn_setup()
    _L0_ffn_in = {k: v for k, v in _L0_ffn_all.items() if k in ('rW1', 'rb1', 'ln_g', 'ln_b', 'rW2', 'rb2', 'qW', 'qb', 'kW', 'kb', 'vW', 'vb', 'oW', 'ob')}
    del _L0_ffn_all

    def _L1_xattn_setup():
        import jax, jax.numpy as jnp
        import numpy as np
        B, S, D_MODEL, N_HEADS = (4, 256, 128, 16)
        HEAD_DIM = D_MODEL // N_HEADS
        key = jax.random.key(seed)
        kq, kk, kv, kw = jax.random.split(key, 4)
        q = jax.random.normal(kq, (B, S, D_MODEL), dtype=jnp.float32)
        k = jax.random.normal(kk, (B, S, D_MODEL), dtype=jnp.float32)
        v = jax.random.normal(kv, (B, S, D_MODEL), dtype=jnp.float32)
        W_out = jax.random.normal(kw, (D_MODEL, D_MODEL), dtype=jnp.float32) * (1.0 / np.sqrt(D_MODEL))
        return {'q': q, 'k': k, 'v': v, 'W_out': W_out}
    _L1_xattn_all = _L1_xattn_setup()
    _L1_xattn_in = {k: v for k, v in _L1_xattn_all.items() if k in ('W_out',)}
    del _L1_xattn_all

    def _L1_ffn_setup():
        import jax, jax.numpy as jnp
        import numpy as np
        import math
        E = 32
        K = 2
        CF = 1.2
        D = 128
        F = 512
        key = jax.random.key(seed)
        ks = jax.random.split(key, 7)
        s = 0.02
        return {'x': jax.random.normal(ks[0], (4, 256, D), jnp.float32), 'gate_w': jax.random.normal(ks[1], (D, E), jnp.float32) * s, 'gate_b': jnp.zeros((E,), jnp.float32), 'w1': jax.random.normal(ks[2], (E, D, F), jnp.float32) * s, 'b1': jnp.zeros((E, F), jnp.float32), 'w2': jax.random.normal(ks[3], (E, F, D), jnp.float32) * s, 'b2': jnp.zeros((E, D), jnp.float32)}
    _L1_ffn_all = _L1_ffn_setup()
    _L1_ffn_in = {k: v for k, v in _L1_ffn_all.items() if k in ('gate_w', 'gate_b', 'w1', 'b1', 'w2', 'b2')}
    del _L1_ffn_all

    def _L2_xattn_setup():
        import jax, jax.numpy as jnp
        import numpy as np
        EMBED_DIM = 128
        NUM_HEADS = 16
        HEAD_DIM = EMBED_DIM // NUM_HEADS
        key = jax.random.key(seed)
        ks = jax.random.split(key, 7)
        B, S, E = (2, 256, EMBED_DIM)
        bound = float(np.sqrt(6.0 / (E + E)))
        mkw = lambda k: jax.random.uniform(k, (E, E), jnp.float32, -bound, bound)
        return {'query': jax.random.normal(ks[0], (B, S, E), jnp.float32), 'key': jax.random.normal(ks[1], (B, S, E), jnp.float32), 'value': jax.random.normal(ks[2], (B, S, E), jnp.float32), 'Wq': mkw(ks[3]), 'Wk': mkw(ks[4]), 'Wv': mkw(ks[5]), 'Wo': mkw(ks[6])}
    _L2_xattn_all = _L2_xattn_setup()
    _L2_xattn_in = {k: v for k, v in _L2_xattn_all.items() if k in ('Wq', 'Wk', 'Wv', 'Wo')}
    del _L2_xattn_all

    def _L2_ffn_setup():
        import jax, jax.numpy as jnp
        import numpy as np
        NUM_EXPERTS = 8
        TOP_K = 2
        D_MODEL = 128
        D_FF = 512
        B, S = (2, 256)
        key = jax.random.key(seed)
        k1, k2, k3, k4 = jax.random.split(key, 4)
        scale_in = 1.0 / np.sqrt(D_MODEL)
        scale_ff = 1.0 / np.sqrt(D_FF)
        return {'hidden_states': jax.random.normal(k1, (B, S, D_MODEL), dtype=jnp.float32), 'gate_w': jax.random.normal(k2, (D_MODEL, NUM_EXPERTS), dtype=jnp.float32) * scale_in, 'w1': jax.random.normal(k3, (NUM_EXPERTS, D_MODEL, D_FF), dtype=jnp.float32) * scale_in, 'w2': jax.random.normal(k4, (NUM_EXPERTS, D_FF, D_MODEL), dtype=jnp.float32) * scale_ff}
    _L2_ffn_all = _L2_ffn_setup()
    _L2_ffn_in = {k: v for k, v in _L2_ffn_all.items() if k in ('gate_w', 'w1', 'w2')}
    del _L2_ffn_all

    def _L3_xattn_setup():
        import jax, jax.numpy as jnp
        import numpy as np
        B, L_ENC, L_DEC, D = (16, 64, 128, 128)
        key = jax.random.key(seed)
        k1, k2, k3, k4, k5, k6 = jax.random.split(key, 6)
        encoder_hc = jax.random.normal(k1, (B, L_ENC, D), dtype=jnp.float32)
        decoder_hq = jax.random.normal(k2, (B, L_DEC, D), dtype=jnp.float32)
        w_sim = jax.random.normal(k3, (3 * D,), dtype=jnp.float32) * 0.02
        b_sim = jax.random.normal(k4, (1,), dtype=jnp.float32) * 0.02
        W_qv = jax.random.normal(k5, (4 * D, D), dtype=jnp.float32) * 0.02
        b_qv = jax.random.normal(k6, (D,), dtype=jnp.float32) * 0.02
        return {'encoder_hc': encoder_hc, 'decoder_hq': decoder_hq, 'w_sim': w_sim, 'b_sim': b_sim, 'W_qv': W_qv, 'b_qv': b_qv}
    _L3_xattn_all = _L3_xattn_setup()
    _L3_xattn_in = {k: v for k, v in _L3_xattn_all.items() if k in ('w_sim', 'b_sim', 'W_qv', 'b_qv')}
    del _L3_xattn_all

    def _L3_ffn_setup():
        import jax, jax.numpy as jnp
        import numpy as np
        D_MODEL = 128
        M = 64
        INNER = 16
        key = jax.random.key(seed)
        ks = jax.random.split(key, 9)

        def init(k, shape, fan_in):
            bound = 1.0 / np.sqrt(fan_in)
            return jax.random.uniform(k, shape, jnp.float32, -bound, bound)
        x = jax.random.normal(ks[0], (16, 512, D_MODEL), dtype=jnp.float32)
        Win = init(ks[1], (D_MODEL, M), D_MODEL)
        bin_ = init(ks[2], (M,), D_MODEL)
        W1 = init(ks[3], (M, INNER), 1)
        b1 = init(ks[4], (M, INNER), 1)
        W2 = init(ks[5], (M, INNER), INNER)
        b2 = init(ks[6], (M,), INNER)
        Wout = init(ks[7], (M, D_MODEL), M)
        bout = init(ks[8], (D_MODEL,), M)
        return {'x': x, 'Win': Win, 'bin_': bin_, 'W1': W1, 'b1': b1, 'W2': W2, 'b2': b2, 'Wout': Wout, 'bout': bout}
    _L3_ffn_all = _L3_ffn_setup()
    _L3_ffn_in = {k: v for k, v in _L3_ffn_all.items() if k in ('Win', 'bin_', 'W1', 'b1', 'W2', 'b2', 'Wout', 'bout')}
    del _L3_ffn_all
    return {'x': x, 'ctx_1024': ctx_1024, 'mask_1x1xSxS2_ik1': mask_1x1xSxS2_ik1, 'g_xattn': g_xattn, 'g_ffn': g_ffn, 'L0_xattn_Wq': _L0_xattn_in['Wq'], 'L0_xattn_Wk': _L0_xattn_in['Wk'], 'L0_xattn_Wv': _L0_xattn_in['Wv'], 'L0_xattn_Wo': _L0_xattn_in['Wo'], 'L0_xattn_bo': _L0_xattn_in['bo'], 'L0_ffn_rW1': _L0_ffn_in['rW1'], 'L0_ffn_rb1': _L0_ffn_in['rb1'], 'L0_ffn_ln_g': _L0_ffn_in['ln_g'], 'L0_ffn_ln_b': _L0_ffn_in['ln_b'], 'L0_ffn_rW2': _L0_ffn_in['rW2'], 'L0_ffn_rb2': _L0_ffn_in['rb2'], 'L0_ffn_qW': _L0_ffn_in['qW'], 'L0_ffn_qb': _L0_ffn_in['qb'], 'L0_ffn_kW': _L0_ffn_in['kW'], 'L0_ffn_kb': _L0_ffn_in['kb'], 'L0_ffn_vW': _L0_ffn_in['vW'], 'L0_ffn_vb': _L0_ffn_in['vb'], 'L0_ffn_oW': _L0_ffn_in['oW'], 'L0_ffn_ob': _L0_ffn_in['ob'], 'L1_xattn_W_out': _L1_xattn_in['W_out'], 'L1_ffn_gate_w': _L1_ffn_in['gate_w'], 'L1_ffn_gate_b': _L1_ffn_in['gate_b'], 'L1_ffn_w1': _L1_ffn_in['w1'], 'L1_ffn_b1': _L1_ffn_in['b1'], 'L1_ffn_w2': _L1_ffn_in['w2'], 'L1_ffn_b2': _L1_ffn_in['b2'], 'L2_xattn_Wq': _L2_xattn_in['Wq'], 'L2_xattn_Wk': _L2_xattn_in['Wk'], 'L2_xattn_Wv': _L2_xattn_in['Wv'], 'L2_xattn_Wo': _L2_xattn_in['Wo'], 'L2_ffn_gate_w': _L2_ffn_in['gate_w'], 'L2_ffn_w1': _L2_ffn_in['w1'], 'L2_ffn_w2': _L2_ffn_in['w2'], 'L3_xattn_w_sim': _L3_xattn_in['w_sim'], 'L3_xattn_b_sim': _L3_xattn_in['b_sim'], 'L3_xattn_W_qv': _L3_xattn_in['W_qv'], 'L3_xattn_b_qv': _L3_xattn_in['b_qv'], 'L3_ffn_Win': _L3_ffn_in['Win'], 'L3_ffn_bin_': _L3_ffn_in['bin_'], 'L3_ffn_W1': _L3_ffn_in['W1'], 'L3_ffn_b1': _L3_ffn_in['b1'], 'L3_ffn_W2': _L3_ffn_in['W2'], 'L3_ffn_b2': _L3_ffn_in['b2'], 'L3_ffn_Wout': _L3_ffn_in['Wout'], 'L3_ffn_bout': _L3_ffn_in['bout']}

def reference(x, ctx_1024, mask_1x1xSxS2_ik1, g_xattn, g_ffn, L0_xattn_Wq, L0_xattn_Wk, L0_xattn_Wv, L0_xattn_Wo, L0_xattn_bo, L0_ffn_rW1, L0_ffn_rb1, L0_ffn_ln_g, L0_ffn_ln_b, L0_ffn_rW2, L0_ffn_rb2, L0_ffn_qW, L0_ffn_qb, L0_ffn_kW, L0_ffn_kb, L0_ffn_vW, L0_ffn_vb, L0_ffn_oW, L0_ffn_ob, L1_xattn_W_out, L1_ffn_gate_w, L1_ffn_gate_b, L1_ffn_w1, L1_ffn_b1, L1_ffn_w2, L1_ffn_b2, L2_xattn_Wq, L2_xattn_Wk, L2_xattn_Wv, L2_xattn_Wo, L2_ffn_gate_w, L2_ffn_w1, L2_ffn_w2, L3_xattn_w_sim, L3_xattn_b_sim, L3_xattn_W_qv, L3_xattn_b_qv, L3_ffn_Win, L3_ffn_bin_, L3_ffn_W1, L3_ffn_b1, L3_ffn_W2, L3_ffn_b2, L3_ffn_Wout, L3_ffn_bout):
    import jax
    import jax.numpy as jnp

    def _L0_xattn_ref(q, k, v, mask, Wq, Wk, Wv, Wo, bo):
        import jax, jax.numpy as jnp
        import numpy as np
        EMBED = 128
        HEADS = 16
        HEAD_DIM = EMBED // HEADS
        B, S = (4, 256)
        N, qlen = (q.shape[0], q.shape[1])
        klen, vlen = (k.shape[1], v.shape[1])
        qh = q.reshape(N, qlen, HEADS, HEAD_DIM)
        kh = k.reshape(N, klen, HEADS, HEAD_DIM)
        vh = v.reshape(N, vlen, HEADS, HEAD_DIM)
        qh = jnp.einsum('nqhd,ed->nqhe', qh, Wq)
        kh = jnp.einsum('nkhd,ed->nkhe', kh, Wk)
        vh = jnp.einsum('nkhd,ed->nkhe', vh, Wv)
        energy = jnp.einsum('nqhd,nkhd->nhqk', qh, kh)
        energy = jnp.where(mask == 0, jnp.float32(-1e+20), energy)
        attention = jax.nn.softmax(energy / jnp.float32(EMBED ** 0.5), axis=3)
        out = jnp.einsum('nhqk,nkhd->nqhd', attention, vh)
        out = out.reshape(N, qlen, EMBED)
        return out @ Wo.T + bo

    def _L0_ffn_ref(x, rW1, rb1, ln_g, ln_b, rW2, rb2, qW, qb, kW, kb, vW, vb, oW, ob):
        import jax, jax.numpy as jnp
        import numpy as np
        H = 16
        TOP_K = 2
        LN_EPS = 1e-05
        B, S, E = x.shape
        NE = qW.shape[0]
        Dh = E // H
        scale = 1.0 / jnp.sqrt(jnp.asarray(Dh, x.dtype))
        h = x @ rW1.T + rb1
        mu = h.mean(-1, keepdims=True)
        var = ((h - mu) ** 2).mean(-1, keepdims=True)
        h = (h - mu) * jax.lax.rsqrt(var + LN_EPS) * ln_g + ln_b
        h = jax.nn.relu(h)
        logits = h @ rW2.T + rb2
        probs = jax.nn.softmax(logits, axis=-1)
        tp, ti = jax.lax.top_k(probs, TOP_K)
        tp = tp / tp.sum(-1, keepdims=True)
        expert_mask = (jax.nn.one_hot(ti, NE, dtype=probs.dtype) * tp[..., None]).sum(-2)
        gates = jnp.moveaxis(expert_mask, -1, 0)

        def expert_step(acc, params):
            qw, qb_, kw, kb_, vw, vb_, ow, ob_, g = params
            q = (x @ qw.T + qb_).reshape(B, S, H, Dh).transpose(0, 2, 1, 3)
            k = (x @ kw.T + kb_).reshape(B, S, H, Dh).transpose(0, 2, 1, 3)
            v = (x @ vw.T + vb_).reshape(B, S, H, Dh).transpose(0, 2, 1, 3)
            scores = jnp.einsum('bhqd,bhkd->bhqk', q, k) * scale
            p = jax.nn.softmax(scores, axis=-1)
            o = jnp.einsum('bhqk,bhkd->bhqd', p, v)
            o = o.transpose(0, 2, 1, 3).reshape(B, S, E) @ ow.T + ob_
            return (acc + o * g[..., None], None)
        out, _ = jax.lax.scan(expert_step, jnp.zeros_like(x), (qW, qb, kW, kb, vW, vb, oW, ob, gates))
        return out

    def _L1_xattn_ref(q, k, v, W_out):
        import jax, jax.numpy as jnp
        import numpy as np
        B, S, D_MODEL, N_HEADS = (4, 256, 128, 16)
        HEAD_DIM = D_MODEL // N_HEADS
        scale = 1.0 / jnp.sqrt(jnp.float32(HEAD_DIM))
        scores = jnp.einsum('bqd,bkd->bqk', q, k) * scale
        attn = jax.nn.softmax(scores, axis=-1)
        out = jnp.einsum('bqk,bkd->bqd', attn, v)
        return jnp.einsum('bsd,ed->bse', out, W_out)

    def _L1_ffn_ref(x, gate_w, gate_b, w1, b1, w2, b2):
        import jax, jax.numpy as jnp
        import numpy as np
        import math
        E = 32
        K = 2
        CF = 1.2
        D = 128
        F = 512
        orig_shape = x.shape
        xt = x.reshape(-1, D)
        T = xt.shape[0]
        C = int(math.ceil(T * K / E * CF))
        logits = xt @ gate_w + gate_b
        probs = jax.nn.softmax(logits, axis=-1)
        top_w, top_i = jax.lax.top_k(probs, K)
        w = top_w / jnp.sum(top_w, axis=-1, keepdims=True)
        flat_e = top_i.reshape(-1)
        oh = jax.nn.one_hot(flat_e, E, dtype=jnp.int32)
        pos_all = jnp.cumsum(oh, axis=0) - 1
        pos = jnp.take_along_axis(pos_all, flat_e[:, None], axis=1)[:, 0]
        valid = pos < C
        pos_d = jnp.where(valid, pos, C)
        x_rep = jnp.repeat(xt, K, axis=0)
        xe = jnp.zeros((E, C, D), x.dtype).at[flat_e, pos_d].add(x_rep, mode='drop')
        he = jax.nn.gelu(jnp.einsum('ecd,edf->ecf', xe, w1) + b1[:, None, :], approximate=False)
        ye = jnp.einsum('ecf,efd->ecd', he, w2) + b2[:, None, :]
        y_flat = ye[flat_e, jnp.minimum(pos, C - 1)] * valid[:, None].astype(x.dtype)
        y = (y_flat.reshape(T, K, D) * w[..., None]).sum(axis=1)
        return y.reshape(orig_shape)

    def _L2_xattn_ref(query, key, value, Wq, Wk, Wv, Wo):
        import jax, jax.numpy as jnp
        import numpy as np
        EMBED_DIM = 128
        NUM_HEADS = 16
        HEAD_DIM = EMBED_DIM // NUM_HEADS
        B, L, E = query.shape
        H, D = (NUM_HEADS, HEAD_DIM)
        scale = D ** (-0.5)
        q = (query @ Wq.T).reshape(B, L, H, D) * scale
        k = (key @ Wk.T).reshape(B, -1, H, D)
        v = (value @ Wv.T).reshape(B, -1, H, D)
        scores = jax.nn.sigmoid(jnp.einsum('blhd,bshd->bhls', q, k))
        o = jnp.einsum('bhls,bshd->blhd', scores, v).reshape(B, L, E)
        return o @ Wo.T

    def _L2_ffn_ref(hidden_states, gate_w, w1, w2):
        import jax, jax.numpy as jnp
        import numpy as np
        NUM_EXPERTS = 8
        TOP_K = 2
        D_MODEL = 128
        D_FF = 512
        B, S = (2, 256)
        b, s, d = hidden_states.shape
        x = hidden_states.reshape(-1, d)
        gate_logits = x @ gate_w
        top_vals, top_idx = jax.lax.top_k(gate_logits, TOP_K)
        top_w = jax.nn.softmax(top_vals.astype(jnp.float32), axis=1).astype(x.dtype)
        combine = jnp.einsum('tke,tk->te', jax.nn.one_hot(top_idx, NUM_EXPERTS, dtype=x.dtype), top_w)
        h = jax.nn.relu(jnp.einsum('td,edf->etf', x, w1))
        expert_out = jnp.einsum('etf,efd->etd', h, w2)
        final = jnp.einsum('etd,te->td', expert_out, combine)
        return final.reshape(b, s, d)

    def _L3_xattn_ref(encoder_hc, decoder_hq, w_sim, b_sim, W_qv, b_qv):
        import jax, jax.numpy as jnp
        import numpy as np
        B, L_ENC, L_DEC, D = (16, 64, 128, 128)
        d = encoder_hc.shape[-1]
        w1, w2, w3 = (w_sim[:d], w_sim[d:2 * d], w_sim[2 * d:])
        Sim = (encoder_hc @ w1)[:, :, None] + (decoder_hq @ w2)[:, None, :] + jnp.einsum('bid,bjd->bij', encoder_hc * w3, decoder_hq) + b_sim[0]
        A = jax.nn.softmax(Sim, axis=2)
        hq_hat = jnp.einsum('bij,bjd->bid', A, decoder_hq)
        Batt = jax.nn.softmax(jnp.max(Sim, axis=2), axis=1)
        hc_bar = jnp.einsum('bi,bid->bd', Batt, encoder_hc)[:, None, :]
        hc_hat = jnp.broadcast_to(hc_bar, encoder_hc.shape)
        feats = jnp.concatenate([encoder_hc, hq_hat, encoder_hc * hq_hat, encoder_hc * hc_hat], axis=-1)
        hcq = feats @ W_qv + b_qv
        return hcq

    def _L3_ffn_ref(x, Win, bin_, W1, b1, W2, b2, Wout, bout):
        import jax, jax.numpy as jnp
        import numpy as np
        D_MODEL = 128
        M = 64
        INNER = 16
        s = jnp.einsum('btd,dm->btm', x, Win) + bin_
        h = jax.nn.relu(s[..., None] * W1 + b1)
        g = jnp.einsum('btmh,mh->btm', h, W2) + b2
        out = jnp.einsum('btm,md->btd', g, Wout) + bout
        return out
    x = x + jnp.tanh(g_xattn[0]) * _L0_xattn_ref(_layernorm(x, axis=-1), ctx_1024, ctx_1024, mask_1x1xSxS2_ik1, L0_xattn_Wq, L0_xattn_Wk, L0_xattn_Wv, L0_xattn_Wo, L0_xattn_bo)
    x = x + jnp.tanh(g_ffn[0]) * _L0_ffn_ref(_layernorm(x, axis=-1), L0_ffn_rW1, L0_ffn_rb1, L0_ffn_ln_g, L0_ffn_ln_b, L0_ffn_rW2, L0_ffn_rb2, L0_ffn_qW, L0_ffn_qb, L0_ffn_kW, L0_ffn_kb, L0_ffn_vW, L0_ffn_vb, L0_ffn_oW, L0_ffn_ob)
    x = x + jnp.tanh(g_xattn[1]) * _L1_xattn_ref(_layernorm(x, axis=-1), ctx_1024, ctx_1024, L1_xattn_W_out)
    x = x + jnp.tanh(g_ffn[1]) * _L1_ffn_ref(_layernorm(x, axis=-1), L1_ffn_gate_w, L1_ffn_gate_b, L1_ffn_w1, L1_ffn_b1, L1_ffn_w2, L1_ffn_b2)
    x = x + jnp.tanh(g_xattn[2]) * _L2_xattn_ref(_layernorm(x, axis=-1), ctx_1024, ctx_1024, L2_xattn_Wq, L2_xattn_Wk, L2_xattn_Wv, L2_xattn_Wo)
    x = x + jnp.tanh(g_ffn[2]) * _L2_ffn_ref(_layernorm(x, axis=-1), L2_ffn_gate_w, L2_ffn_w1, L2_ffn_w2)
    x = x + jnp.tanh(g_xattn[3]) * _L3_xattn_ref(_layernorm(x, axis=-1), ctx_1024, L3_xattn_w_sim, L3_xattn_b_sim, L3_xattn_W_qv, L3_xattn_b_qv)
    x = x + jnp.tanh(g_ffn[3]) * _L3_ffn_ref(_layernorm(x, axis=-1), L3_ffn_Win, L3_ffn_bin_, L3_ffn_W1, L3_ffn_b1, L3_ffn_W2, L3_ffn_b2, L3_ffn_Wout, L3_ffn_bout)
    return x

_drawn_inputs = setup_inputs


def setup_inputs(seed=0):
    import zlib

    import numpy as np

    out = dict(_drawn_inputs(seed))
    spreads = {'L0_ffn_rb1': (0.0, 0.765),
     'L0_ffn_ln_g': (1.0, 0.6),
     'L0_ffn_ln_b': (0.0, 0.8),
     'L0_ffn_rb2': (0.0, 0.525),
     'L0_ffn_qb': (0.0, 0.8),
     'L0_ffn_kb': (0.0, 2.0),
     'L0_ffn_vb': (0.0, 0.8),
     'L0_ffn_ob': (0.0, 0.486),
     'L1_ffn_gate_b': (0.0, 0.717),
     'L1_ffn_b1': (0.0, 0.8),
     'L1_ffn_b2': (0.0, 0.746)}
    factors = {'g_ffn': 8.0,
     'L0_xattn_Wq': 2.949,
     'L0_xattn_Wk': 3.058,
     'L0_xattn_bo': 8.0,
     'L0_ffn_rW1': 4.096,
     'L0_ffn_rW2': 4.108,
     'L0_ffn_qW': 8.0,
     'L0_ffn_kW': 8.0,
     'L0_ffn_vW': 8.0,
     'L0_ffn_oW': 8.0,
     'L1_ffn_gate_w': 4.782,
     'L1_ffn_w1': 8.0,
     'L1_ffn_w2': 8.0,
     'L2_ffn_gate_w': 3.813,
     'L2_ffn_w1': 4.19,
     'L2_ffn_w2': 3.454,
     'L3_xattn_w_sim': 8.0,
     'L3_xattn_W_qv': 3.908,
     'L3_xattn_b_qv': 64.0,
     'L3_ffn_Win': 8.0,
     'L3_ffn_bin_': 8.0,
     'L3_ffn_W1': 8.0,
     'L3_ffn_b1': 8.0,
     'L3_ffn_W2': 8.0,
     'L3_ffn_b2': 25.603,
     'L3_ffn_Wout': 8.0,
     'L3_ffn_bout': 200.0}
    for name, (base, spread) in spreads.items():
        noise = np.random.default_rng([zlib.crc32(name.encode()), seed]).standard_normal(out[name].shape)
        drawn = base * np.exp(spread * noise) if base else spread * noise
        out[name] = jnp.asarray(drawn.astype(out[name].dtype))
    for name, factor in factors.items():
        out[name] = (out[name] * factor).astype(out[name].dtype)
    return out
```

```python
from contextlib import ExitStack

import concourse.bass as bass
from concourse import mybir

F32 = mybir.dt.float32
F16 = mybir.dt.float16
BF16 = mybir.dt.bfloat16
U32 = mybir.dt.uint32
ALU = mybir.AluOpType
ACT = mybir.ActivationFunctionType
AX = mybir.AxisListType

P = 128
B = 64
S = 128
D = 128
NC = 120
T = B * S
HEADS = 16
HD = D // HEADS
E0 = 8
E1, F1, CAP = 32, 512, 615
ROWS1 = -(-CAP // P) * P
E2, F2 = 8, 512
M3, I3 = 64, 16
EPS = 1e-5
MASKED = -1e20

SETS = 4
TERMS = 3
KROWS = TERMS * SETS * HD
MAXROW = KROWS


def strided(ap, offset, dims):
    return bass.AP(tensor=ap.tensor, offset=offset, ap=dims)

STAGES = ('x0', 'f0', 'x1', 'f1', 'x2', 'f2', 'x3', 'f3')


class Core:

    def __init__(self, nc, ctx):
        self.nc, self.ctx, self.names, self.numbers = nc, ctx, {}, set()
        sb = self.sb
        self.x = sb("x", [P, B, D])
        self.xnT = sb("xnT", [P, B * S])
        self.ctxT = sb("ctxT", [P, B * NC])
        self.ident = sb("ident", [P, P])
        self.ident_bf = sb("ident_bf", [P, P], BF16)
        self.tanh_g = sb("tanh_g", [P, 8])
        self.mean = sb("mean", [P, B])
        self.rstd = sb("rstd", [P, B])

    def sb(self, name, shape, dt=F32, ctx=None):
        return (ctx or self.ctx).enter_context(self.nc.sbuf_tensor(self.unique(name), shape, dt))

    def ps(self, name, shape, ctx, dt=F32):
        return ctx.enter_context(self.nc.psum_tensor(self.unique(name), shape, dt))

    def unique(self, name):
        self.names[name] = self.names.get(name, -1) + 1
        return f"{name}_{self.names[name]}" if self.names[name] else name

    def sem(self, name, ctx):
        s = ctx.enter_context(self.nc.semaphore(name))
        self.numbers.add(s.num)
        return s

    def recycle_semaphores(self):
        lo, hi = min(self.numbers), max(self.numbers)
        self.nc.all_engine_barrier(sems_to_clear=range(lo, hi + 1))


def load_inputs(nc, core, inp):
    x, ident = core.x, core.ident
    GB = 4
    steps = B // GB
    with ExitStack() as ctx:
        cbuf = [core.sb(f"cbuf{i}", [NC, GB, D], ctx=ctx) for i in range(2)]
        gates = core.sb("gates", [P, 8], ctx=ctx)
        pc = [core.ps(f"pc{i}", [P, GB * NC], ctx) for i in range(2)]
        s_x, s_g, s_zero, s_ident = (core.sem(n, ctx) for n in ("li_x", "li_g", "li_zero", "li_ident"))
        s_ctx = [core.sem(f"li_ctx{i}", ctx) for i in range(2)]
        s_tr, s_out = (core.sem(n, ctx) for n in ("li_tr", "li_out"))
        with nc.Block() as block:

            @block.sync
            def _(sp):
                sp.dma_start(gates[:, 0:4], inp["g_xattn"].partition_broadcast(P)).then_inc(s_g, 16)
                sp.dma_start(gates[:, 4:8], inp["g_ffn"].partition_broadcast(P)).then_inc(s_g, 16)
                xv = inp["x"].rearrange("b s d -> s b d")
                sp.sem_inc(s_tr, 2)
                with sp.Fori(0, steps // 2) as it:
                    for par in range(2):
                        g = it * 2 + par
                        sp.wait_ge(s_tr, g + 1)
                        sp.dma_start(cbuf[par][:, :, :], inp["ctx_1024"][bass.ds(g * GB, GB), :, :]
                                     .rearrange("b s d -> s b d")).then_inc(s_ctx[par], 16)
                        sp.dma_start(x[:, bass.ds(g * GB, GB), :], xv[:, bass.ds(g * GB, GB), :]).then_inc(s_x, 16)
                sp.wait_ge(s_x, 16 * steps)

            @block.gpsimd
            def _(pool):
                pool.memset(ident[:, :], 0.0).then_inc(s_zero, 1)
                pool.wait_ge(s_zero, 1)
                pool.affine_select(out=ident[:, :], in_=ident[:, :], compare_op=ALU.not_equal, fill=1.0, base=0,
                                   pattern=[[-1, P]], channel_multiplier=1).then_inc(s_ident, 1)
                pool.wait_ge(s_ident, 1)
                pool.tensor_copy(core.ident_bf[:, :], ident[:, :]).then_inc(s_ident, 1)
                pool.wait_ge(s_ident, 2)

            @block.tensor
            def _(pe):
                pe.wait_ge(s_ident, 1)
                pe.sem_inc(s_out, 2)
                with pe.Fori(0, steps // 2) as it:
                    for par in range(2):
                        g = it * 2 + par
                        pe.wait_ge(s_ctx[par], it * 16 + 16)
                        pe.wait_ge(s_out, g + 1)
                        for j in range(GB):
                            mm = pe.transpose(pc[par][:, j * NC:(j + 1) * NC], cbuf[par][:, j, :], ident[0:NC, 0:NC])
                        mm.then_inc(s_tr, 1)

            @block.scalar
            def _(act):
                act.wait_ge(s_g, 32)
                act.activation(core.tanh_g[:, :], gates[:, :], ACT.Tanh).then_inc(s_g, 1)
                act.wait_ge(s_g, 33)
                with act.Fori(0, steps // 2) as it:
                    for par in range(2):
                        g = it * 2 + par
                        act.wait_ge(s_tr, g + 3)
                        act.activation(core.ctxT[:, bass.ds(g * (GB * NC), GB * NC)], pc[par][:, :],
                                       ACT.Copy).then_inc(s_out, 1)
                act.wait_ge(s_out, steps + 2)


def layernorm_transpose(nc, core, name):
    x = core.x
    GB = 4
    steps = B // GB
    PARTS = 4
    N, PER = B // PARTS, steps // PARTS
    with ExitStack() as ctx:
        stats = core.sb("stats", [P, B, 6], ctx=ctx)
        tmp = [core.sb(f"ln_tmp{i}", [P, B], ctx=ctx) for i in range(3)]
        std = core.sb("ln_std", [P, B], ctx=ctx)
        shift = core.sb("ln_shift", [P, B], ctx=ctx)
        xn = [core.sb(f"xn{i}", [P, GB, D], ctx=ctx) for i in range(2)]
        pT = [core.ps(f"pT{i}", [P, GB * S], ctx) for i in range(2)]
        s_st, s_ar, s_std, s_rstd, s_xn_dve, s_xn_act, s_tr, s_out = (
            core.sem(f"{name}_{n}", ctx) for n in ("st", "ar", "std", "rstd", "xn_dve", "xn_act", "tr", "out"))
        with nc.Block() as block:

            @block.vector
            def _(dve):
                def moments(part):
                    cols = bass.ds(part * N, N)
                    for j in range(N):
                        dve.bn_stats(stats[:, part * N + j, :], x[:, part * N + j, :]).then_inc(s_st, 1)
                    dve.wait_ge(s_st, part * N + N)
                    me, mo = stats[:, cols, 1], stats[:, cols, 4]
                    t = [v[:, cols] for v in tmp]
                    dve.tensor_tensor(t[0], me, mo, ALU.add).then_inc(s_ar, 1)
                    dve.tensor_tensor(t[1], me, mo, ALU.subtract).then_inc(s_ar, 1)
                    dve.tensor_tensor(t[2], stats[:, cols, 2], stats[:, cols, 5], ALU.add).then_inc(s_ar, 1)
                    dve.wait_ge(s_ar, part * 7 + 3)
                    dve.tensor_scalar(core.mean[:, cols], t[0], 0.5, None, ALU.mult).then_inc(s_ar, 1)
                    dve.scalar_tensor_tensor(t[1], t[1], 0.25, t[1], ALU.mult, ALU.mult).then_inc(s_ar, 1)
                    dve.tensor_scalar(t[2], t[2], 1.0 / D, EPS, ALU.mult, ALU.add).then_inc(s_ar, 1)
                    dve.wait_ge(s_ar, part * 7 + 6)
                    dve.tensor_tensor(t[0], t[1], t[2], ALU.add).then_inc(s_ar, 1)

                def invert(part):
                    cols = bass.ds(part * N, N)
                    dve.wait_ge(s_std, part + 1)
                    dve.reciprocal(core.rstd[:, cols], std[:, cols]).then_inc(s_rstd, 1)
                    dve.wait_ge(s_rstd, part * 5 + 1)
                    r, t = core.rstd[:, cols], tmp[1][:, cols]
                    dve.scalar_tensor_tensor(t, r, -0.5, r, ALU.mult, ALU.mult).then_inc(s_rstd, 1)
                    dve.wait_ge(s_rstd, part * 5 + 2)
                    dve.tensor_tensor(t, t, tmp[0][:, cols], ALU.mult).then_inc(s_rstd, 1)
                    dve.wait_ge(s_rstd, part * 5 + 3)
                    dve.scalar_tensor_tensor(r, t, 1.5, r, ALU.add, ALU.mult).then_inc(s_rstd, 1)
                    dve.wait_ge(s_rstd, part * 5 + 4)
                    dve.scalar_tensor_tensor(shift[:, cols], core.mean[:, cols], -1.0, r, ALU.mult,
                                             ALU.mult).then_inc(s_rstd, 1)
                    dve.wait_ge(s_rstd, part * 5 + 5)

                def apply(part):
                    for k in range(PER):
                        g = part * PER + k
                        dve.wait_ge(s_tr, g + 1)
                        for j in range(2):
                            b = g * GB + j
                            ins = dve.tensor_scalar(xn[k % 2][:, j, :], x[:, b, :], core.mean[:, bass.ds(b, 1)],
                                                    core.rstd[:, bass.ds(b, 1)], ALU.subtract, ALU.mult)
                        ins.then_inc(s_xn_dve, 1)

                dve.sem_inc(s_tr, 2)
                moments(0)
                invert(0)
                with dve.Fori(0, PARTS - 1) as part:
                    moments(part + 1)
                    apply(part)
                    invert(part + 1)
                apply(PARTS - 1)

            @block.tensor
            def _(pe):
                pe.sem_inc(s_out, 2)
                with pe.Fori(0, steps // 2) as it:
                    for par in range(2):
                        g = it * 2 + par
                        pe.wait_ge(s_xn_dve, g + 1)
                        pe.wait_ge(s_xn_act, g + 1)
                        pe.wait_ge(s_out, g + 1)
                        for j in range(GB):
                            mm = pe.transpose(pT[par][:, j * S:(j + 1) * S], xn[par][:, j, :], core.ident[:, :])
                        mm.then_inc(s_tr, 1)

            @block.scalar
            def _(act):
                def root(part):
                    act.wait_ge(s_ar, part * 7 + 7)
                    cols = bass.ds(part * N, N)
                    act.activation(std[:, cols], tmp[0][:, cols], ACT.Sqrt).then_inc(s_std, 1)

                def take(g, par):
                    act.wait_ge(s_tr, g + 3)
                    act.activation(core.xnT[:, bass.ds(g * (GB * S), GB * S)], pT[par][:, :],
                                   ACT.Copy).then_inc(s_out, 1)

                def apply(part):
                    act.wait_ge(s_rstd, part * 5 + 5)
                    for k in range(PER):
                        g = part * PER + k
                        act.wait_ge(s_tr, g + 1)
                        for j in range(2, GB):
                            b = g * GB + j
                            ins = act.activation(xn[k % 2][:, j, :], x[:, b, :], ACT.Identity,
                                                 bias=shift[:, bass.ds(b, 1)], scale=core.rstd[:, bass.ds(b, 1)])
                        ins.then_inc(s_xn_act, 1)
                        if not isinstance(g, int) or g > 0:
                            take(g - 1, (k - 1) % 2)

                root(0)
                root(1)
                apply(0)
                with act.Fori(1, PARTS - 1) as part:
                    root(part + 1)
                    apply(part)
                apply(PARTS - 1)
                take(steps - 1, (steps - 1) % 2)
                act.wait_ge(s_out, steps + 2)


def store_output(nc, core, out):
    with ExitStack() as ctx:
        s_st = core.sem("so_store", ctx)
        with nc.Block() as block:

            @block.sync
            def _(sp):
                ov = out.rearrange("b s d -> s b d")
                for g in range(4):
                    sp.dma_start(ov[:, 16 * g:16 * g + 16, :], core.x[:, 16 * g:16 * g + 16, :]).then_inc(s_st, 16)
                sp.wait_ge(s_st, 64)


def head_attention(nc, core, name, wq, wk, wv, wo, scale, bias=None, mask=None, ctx_keys=True, experts=1,
                   gate=None, coef=None, sigmoid=False):
    NK = NC if ctx_keys else S
    PAIRS = B // 2
    U = B
    DMAS = 1 + 4
    softmax = not sigmoid
    krows = KROWS + 1 if softmax and mask is None else KROWS
    x, ident = core.x, core.ident
    with ExitStack() as ctx:
        def sb(n, shape, dt=F32):
            return core.sb(f"{name}_{n}", shape, dt, ctx)

        def sem(n):
            return core.sem(f"{name}_{n}", ctx)

        w_q, w_k, w_v = sb("w_q", [D, D]), sb("w_k", [D, D]), sb("w_v", [D, D])
        w_o = sb("w_o", [P, 2, D])
        xs = [sb(f"xs{i}", [D, 2 * S]) for i in range(2)]
        kvs = [sb(f"kvs{i}", [D, 2 * NC]) for i in range(2)] if ctx_keys else xs
        q_half = sb("q_half", [P, 2, 2 * S], F16)
        k_half = sb("k_half", [P, 2, 2 * NK], F16)
        zeros = sb("zeros", [P, 2 * S])
        q_full, k_full = sb("q_full", [P, 2 * S]), sb("k_full", [P, 2 * NK])
        kst = [sb(f"kst{i}", [P, SETS, 2, NK], F16) for i in range(2)]
        qbd = [sb(f"qbd{i}", [P, SETS, 4, 2, S], F16) for i in range(2)]
        vpad = [[sb(f"vpad{i}{j}", [P, SETS, 4, 32]) for j in range(2)] for i in range(2)]
        probs = [sb(f"probs{i}", [P, SETS, 4 * S]) for i in range(2)]
        o_sb = sb("o_sb", [P, 2 * S])
        if softmax:
            rowmax = [sb(f"rowmax{i}", [P, HEADS]) for i in range(2)]
            negmax = sb("negmax", [HEADS, S], BF16 if mask is not None else F16)
            sums = sb("sums", [P, S])
            recip = sb("recip", [P, S])
            is_sum = sb("is_sum", [P, 2])
            sum_last = sb("sum_last", [P, 32])
            o_norm = sb("o_norm", [P, 2 * S])
            spread = sb("spread", [P, 2, P])
        if mask is not None:
            maskraw = sb("maskraw", [P, NC], mybir.dt.int32)
            maskneg = sb("maskneg", [P, NC], BF16)
            ones_row = sb("ones_row", [1, NC], BF16)
            maxrow = [sb(f"maxrow{i}", [1, HEADS, S], BF16) for i in range(2)]
        if bias is not None:
            b_q, b_k, b_v = sb("b_q", [P, 1]), sb("b_k", [P, 1]), sb("b_v", [P, 2])

        k_dram = nc.dram_tensor(f"{name}_k_dram", (2, TERMS, P, 2 * NK), F16, kind="Internal").ap()
        q_dram = nc.dram_tensor(f"{name}_q_dram", (2, TERMS, P, 2 * S), F16, kind="Internal").ap()

        ps_misc = core.ps(f"{name}_ps_misc", [P, 512], ctx)
        ps_o = core.ps(f"{name}_ps_o", [P, 512], ctx)
        ps_sum = core.ps(f"{name}_ps_sum", [P, 512], ctx)
        ps_s = [core.ps(f"{name}_ps_s{i}", [P, 512], ctx) for i in range(2)]
        ps_st = [core.ps(f"{name}_ps_st{i}", [P, 512], ctx) for i in range(3)]
        ps_qk = ps_s[0]
        ps_v, ps_mt, ps_out = ps_misc[:, 0:256], ps_misc[0:HEADS, 256:384], ps_misc[:, 384:512]

        s_init, s_w, s_xs, s_qk, s_qhi, s_khi, s_qlo, s_klo = (
            sem(n) for n in ("init", "w", "xs", "qk", "qhi", "khi", "qlo", "klo"))
        s_stack = [sem(f"stack{i}") for i in range(2)]
        s_pv, s_v, s_score, s_max, s_mt, s_neg, s_negd, s_st, s_prob = (
            sem(n) for n in ("pv", "v", "score", "max", "mt", "neg", "negd", "st", "prob"))
        s_bounce, s_sumc = sem("bounce"), sem("sumc")
        s_av, s_o, s_sum, s_rec, s_norm, s_out, s_upd = (
            sem(n) for n in ("av", "o", "sum", "rec", "norm", "out", "upd"))
        AHEAD = {id(s_qlo): 1, id(s_klo): 1, id(s_pv): 2, id(s_v): 3, id(s_max): 2, id(s_mt): 2,
                 id(s_neg): 2, id(s_negd): 1, id(s_st): 9, id(s_prob): 9, id(s_av): 3, id(s_o): 1, id(s_rec): 1,
                 id(s_norm): 1, id(s_out): 1, id(s_upd): 4, id(s_sumc): 1, id(s_bounce): 1, id(s_qk): 0}

        def cnt(s, n):
            return n + AHEAD.get(id(s), 0)

        wdma, wo_dma = (3, 1) if bias is None else (5, 2)
        s_fold, s_wo, s_wo_in, s_turn = sem("fold"), sem("wo"), sem("wo_in"), sem("turn")
        s_mask, s_pad, s_qke = sem("mask"), sem("pad"), sem("qke")
        s_set = sem("set")
        INIT = 1 + 32 * softmax + 16 * (mask is not None)
        FREE = (s_sumc, s_bounce, s_qlo, s_klo, s_pv, s_v, s_max, s_mt, s_neg, s_negd, s_st, s_prob, s_av, s_o, s_rec, s_norm,
                s_out, s_upd)

        def steps(eng, slot, first):
            def body(e):
                for k in range(4):
                    slot(e * U + k, e * PAIRS + k // 2, k // 2, k, k, True, k >= 1, k >= 2, k >= 3, 2, e)
                with eng.Fori(1, U // 4 - 1) as it:
                    for j in range(4):
                        slot(e * U + it * 4 + j, e * PAIRS + it * 2 + j // 2, it * 2 + j // 2, it * 4 + j, j, True, True, True, True,
                             2, e)
                for j in range(4):
                    slot(e * U + (U - 4 + j), e * PAIRS + (PAIRS - 2 + j // 2), PAIRS - 2 + j // 2, U - 4 + j, j, True, True, True, True,
                         1 if j < 2 else 0, e)

            def tail(e):
                for j in range(3):
                    slot(e * U + (U + j), e * PAIRS + PAIRS, PAIRS, U + j, j, False, j < 1, j < 2, True, 0, e)
            first(0)
            if experts > 1:
                with eng.Fori(0, experts - 1) as e:
                    body(e)
                    first(e + 1)
                    tail(e)
            body(experts - 1)
            tail(experts - 1)

        with nc.Block() as block:

            @block.sync
            def _(sp):
                for s in FREE:
                    sp.sem_inc(s, AHEAD[id(s)])
                if softmax:
                    sp.dma_start(spread[:, :, :], core.inp["spread"]).then_inc(s_init, 16)
                    sp.dma_start(is_sum[:, :], core.inp["is_sum"]).then_inc(s_init, 16)
                if mask is not None:
                    sp.dma_start(maskraw[:, :], mask).then_inc(s_init, 16)

                def stack_pair(pr, par):
                    sp.wait_ge(s_qlo, cnt(s_qlo, pr + 1))
                    sp.wait_ge(s_klo, cnt(s_klo, pr + 1))
                    sp.dma_start(k_dram[par, 0:2].rearrange("a p n -> p a n"), k_half[:, :, :]).then_inc(s_bounce, 16)
                    sp.dma_start(k_dram[par, 2], k_half[:, 0, :]).then_inc(s_bounce, 16)
                    sp.dma_start(q_dram[par, 1:3].rearrange("a p n -> p a n"), q_half[:, :, :]).then_inc(s_bounce, 16)
                    sp.dma_start(q_dram[par, 0], q_half[:, 0, :]).then_inc(s_bounce, 16)
                    sp.wait_ge(s_bounce, cnt(s_bounce, (pr + 1) * 64))
                    sp.wait_ge(s_st, cnt(s_st, pr * 8 - 8))
                    sp.dma_start(kst[par][0:KROWS, :, :, :].rearrange("p t i k -> p (t i k)"),
                                 k_dram[par].rearrange("a (r t) n -> (a r) (t n)", t=SETS)).then_inc(s_stack[par], 16)
                    for s in range(4):
                        src = q_dram[par].rearrange("a (d s t) n -> s (a d) t n", s=4, t=SETS)[s]
                        sp.dma_start(qbd[par][s:KROWS:4, :, s, :, :].rearrange("p t i q -> p t (i q)"), src
                                     ).then_inc(s_stack[par], 16)

                def first(e):
                    if not isinstance(e, int):
                        for s, n in ((s_qk, PAIRS), (s_qke, 2 * PAIRS), (s_pv, PAIRS)):
                            sp.wait_ge(s, cnt(s, e * n))
                            sp.sem_inc(s_turn, 1)
                    for w, d in ((w_q, wq), (w_k, wk), (w_v, wv)):
                        sp.dma_start(w[:, :], d[bass.ds(e, 1), :, :].rearrange("a i o -> (a i) o")).then_inc(s_w, 16)
                    if bias is not None:
                        sp.dma_start(b_q[:, :], bias[0][bass.ds(e, 1), :].rearrange("a n -> n a")).then_inc(s_w, 16)
                        sp.dma_start(b_k[:, :], bias[1][bass.ds(e, 1), :].rearrange("a n -> n a")).then_inc(s_w, 16)
                    stack_pair(e * PAIRS, 0)
                    sp.wait_ge(s_upd, cnt(s_upd, e * U))
                    sp.sem_inc(s_turn, 1)
                    sp.dma_start(w_o[:, :, :], wo[bass.ds(e, 1), :, :, :].rearrange("a h p n -> (a p) h n")
                                 ).then_inc(s_wo_in, 16)
                    if bias is not None:
                        sp.dma_start(b_v[:, :], bias[2][bass.ds(e, 1), :, :].rearrange("a p h -> (a p) h")
                                     ).then_inc(s_wo_in, 16)

                def slot(u, pr, kp, k, j, scores, soft, values, output, next_pair, e):
                    par, i = j // 2, j % 2
                    if i == 0 and next_pair:
                        stack_pair(pr + 1, 1 - par)

                steps(sp, slot, first)

            @block.gpsimd
            def _(pool):
                clears = [(zeros[:, :], 0.0)]
                for i in range(2):
                    clears.append((qbd[i][:, :, :, :, :], 0.0))
                    if softmax and mask is None:
                        clears.append((kst[i][MAXROW:MAXROW + 1, :, :, :], 1.0))
                    for j in range(2):
                        clears.append((vpad[i][j][:, :, :, :], 0.0))
                if mask is not None:
                    clears.append((ones_row[:, :], 1.0))
                for n, (dst, value) in enumerate(clears):
                    pool.memset(dst, value).then_inc(s_set, 1)
                    pool.wait_ge(s_set, n + 1)
                pool.sem_inc(s_init, 1)

                def copy_pair(pr, kp, par):
                    pool.wait_ge(s_pv, cnt(s_pv, pr - 1))
                    todo = [(xs, core.xnT, 2 * S)] + ([(kvs, core.ctxT, 2 * NC)] if ctx_keys else [])
                    for dst, src, n in todo:
                        if isinstance(kp, int):
                            pool.tensor_tensor(dst[par][:, :], src[:, kp * n:(kp + 1) * n], zeros[:, 0:n],
                                               ALU.add).then_inc(s_xs, 1)
                        else:
                            pool.tensor_copy(dst[par][:, :], src[:, bass.ds(kp * n, n)]).then_inc(s_xs, 1)

                def first(e):
                    copy_pair(e * PAIRS, 0, 0)
                    copy_pair(e * PAIRS + 1, 1, 1)
                    for n in range(2):
                        make_half(e * PAIRS + n, 0, q_full, q_half, s_qhi, s_qlo)
                        make_half(e * PAIRS + n, 1, k_full, k_half, s_khi, s_klo)

                pool.wait_ge(s_init, INIT)

                def make_half(pr, n, src, half, made, low):
                    if n == 0:
                        pool.wait_ge(s_qke, pr * 2 + 2)
                        pool.wait_ge(s_bounce, cnt(s_bounce, pr * 64))
                    pool.tensor_tensor(half[:, 0, :], src[:, :], zeros[:, 0:src.shape[1]], ALU.add).then_inc(made, 1)
                    pool.wait_ge(made, pr + 1)
                    pool.tensor_tensor(half[:, 1, :], src[:, :], half[:, 0, :], ALU.subtract).then_inc(low, 1)

                def slot(u, pr, kp, k, j, scores, soft, values, output, next_pair, e):
                    if j % 2 == 0 and next_pair == 2:
                        copy_pair(pr + 2, kp + 2, j // 2)
                    if j % 2 == 1 and next_pair == 2:
                        make_half(pr + 2, 0, q_full, q_half, s_qhi, s_qlo)
                        make_half(pr + 2, 1, k_full, k_half, s_khi, s_klo)

                steps(pool, slot, first)

            n_xs = 2 if ctx_keys else 1

            @block.tensor
            def _(pe):
                def project_qk(pr, par, u=None):
                    pe.wait_ge(s_xs, (pr + 1) * n_xs)
                    if u is not None and softmax:
                        pe.wait_ge(s_max, cnt(s_max, u * 4 + 3))
                    pe.wait_ge(s_qlo, cnt(s_qlo, pr))
                    pe.wait_ge(s_klo, cnt(s_klo, pr))
                    pe.matmul(ps_qk[:, 0:2 * S], w_q[:, :], xs[par][:, :], start=True, stop=True)
                    pe.matmul(ps_qk[:, 256:256 + 2 * NK], w_k[:, :], kvs[par][:, :], start=True,
                              stop=True).then_inc(s_qk, 1)

                def transpose_maxima(u, pr, i, j):
                    pe.wait_ge(s_v, cnt(s_v, pr * 2 + 2 * i))
                    pe.wait_ge(s_upd, cnt(s_upd, u - 3))
                    pe.wait_ge(s_max, cnt(s_max, u * 4))
                    pe.transpose(ps_mt, rowmax[(j - 1) % 2][:, :], ident[:, :]).then_inc(s_mt, 1)

                def project_v(u, pr, par, soft, output):
                    pe.wait_ge(s_upd, cnt(s_upd, u - 3))
                    if soft and softmax:
                        pe.wait_ge(s_neg, cnt(s_neg, u))
                    for i in range(2):
                        mm = pe.matmul(ps_v[0:NK, i * D:(i + 1) * D], kvs[par][:, i * NK:(i + 1) * NK], w_v[:, :],
                                       start=True, stop=True)
                    mm.then_inc(s_pv, 1)

                def score(u, c, j):
                    par, i, bank = j // 2, j % 2, ps_s[c % 2]
                    pe.wait_ge(s_max, cnt(s_max, u * 4 + c - 1))
                    if mask is not None:
                        pe.matmul(bank[:, 0:4 * NK], core.ident_bf[:, :],
                                  strided(maskneg[:, :], 0, [[NC, P], [0, 4], [1, NC]]), start=True, stop=False,
                                  skip_group_check=True)
                    for s in range(4):
                        mm = pe.matmul(bank[:, s * NK:(s + 1) * NK], qbd[par][0:KROWS, c, s, i, :],
                                       kst[par][0:KROWS, c, i, :], start=mask is None, stop=True,
                                       skip_group_check=mask is not None)
                    mm.then_inc(s_score, 1)

                def score_t(u, c, j):
                    par, i, bank = j // 2, j % 2, ps_st[c % 3]
                    if c == 0 and softmax:
                        pe.wait_ge(s_negd, cnt(s_negd, (u + 1) * 16))
                    pe.wait_ge(s_prob, cnt(s_prob, u * 4 + (1 if c == 3 else 0)))
                    out = bank[0:NK, :]
                    mm = pe.matmul(out, kst[par][0:krows, c, i, :], qbd[par][0:krows, c, :, i, :], start=True,
                                   stop=mask is None, skip_group_check=mask is not None)
                    if mask is not None:
                        pe.matmul(out, maskneg[:, :], strided(core.ident_bf[:, :], 0, [[P, P], [0, 4], [1, P]]),
                                  start=False, stop=False, skip_group_check=True)
                        mm = pe.matmul(out, ones_row[:, :], maxrow[i][:, 4 * c:4 * c + 4, :], start=False, stop=True,
                                       skip_group_check=True)
                    mm.then_inc(s_st, 1)

                def weigh(u, c, j):
                    par, i = j // 2, j % 2
                    pe.wait_ge(s_prob, cnt(s_prob, u * 4 + c + 1))
                    if c == 0:
                        pe.wait_ge(s_o, cnt(s_o, u))
                    half = 0 if c < 3 else 1
                    for s in range(4):
                        mm = pe.matmul(ps_o[32 * s:32 * s + 32, half * S:half * S + S], vpad[par][i][0:NK, c, s, :],
                                       probs[i][0:NK, c, s * S:(s + 1) * S], start=c == 0, stop=c == 3,
                                       skip_group_check=True)
                    if c == 3 and softmax:
                        for s in range(4):
                            mm = pe.matmul(ps_o[32 * s:32 * s + 32, 0:S], sum_last[0:NK, :],
                                           probs[i][0:NK, c, s * S:(s + 1) * S], start=False, stop=True,
                                           skip_group_check=True)
                    if c == 3:
                        mm.then_inc(s_av, 1)

                def spread_sums(u):
                    pe.wait_ge(s_norm, cnt(s_norm, u))
                    pe.wait_ge(s_rec, cnt(s_rec, u + 1))
                    for half in range(2):
                        mm = pe.matmul(ps_sum[:, half * S:(half + 1) * S], spread[:, half, :], recip[:, :],
                                       start=True, stop=True)
                    mm.then_inc(s_sum, 1)

                def project_out(u):
                    src, ready = (o_norm, s_norm) if softmax else (o_sb, s_o)
                    pe.wait_ge(ready, cnt(ready, u + 1))
                    pe.wait_ge(s_upd, cnt(s_upd, u))
                    for half in range(2):
                        mm = pe.matmul(ps_out, src[:, half * S:(half + 1) * S], w_o[:, half, :], start=half == 0,
                                       stop=half == 1)
                    mm.then_inc(s_out, 1)

                pe.wait_ge(s_init, INIT)
                if softmax:
                    pe.wait_ge(s_pad, 10)
                if mask is not None:
                    pe.wait_ge(s_mask, 1)

                def first(e):
                    pe.wait_ge(s_w, (e + 1) * (16 * wdma))
                    project_qk(e * PAIRS, 0, None if isinstance(e, int) else e * U - 1)
                    project_qk(e * PAIRS + 1, 1)

                def fold_bias(e):
                    for half in range(2):
                        mm = pe.matmul(ps_out[0:1, :], b_v[:, half:half + 1], w_o[:, half, :], start=half == 0,
                                       stop=half == 1)
                    mm.then_inc(s_fold, 1)

                def slot(u, pr, kp, k, j, scores, soft, values, output, next_pair, e):
                    par, i = j // 2, j % 2
                    if bias is not None and isinstance(k, int) and k == 2:
                        pe.wait_ge(s_wo, e + 1)
                    if i == 0 and scores:
                        pe.wait_ge(s_stack[par], (pr - par) * (8 * DMAS) + 16 * DMAS)
                    if soft and softmax:
                        transpose_maxima(u, pr, i if scores else 0, j)
                    if scores and softmax:
                        if i == 0:
                            pe.wait_ge(s_qke, (pr + (2 if next_pair else 1)) * 2)
                        score(u, 0, j)
                        score(u, 1, j)
                    for c in range(SETS):
                        if c == 3 and soft:
                            score_t(u - 1, 0, (j - 1) % 4)
                        if values:
                            weigh(u - 2, c, (j - 2) % 4)
                        if c == 0 and output and softmax:
                            spread_sums(u - 3)
                        if scores and softmax and c < 2:
                            score(u, c + 2, j)
                        if c == 0 and i == 0 and scores:
                            project_v(u, pr, par, soft, output)
                        if c == 2 and i == 1 and next_pair == 2:
                            project_qk(pr + 2, par, u)
                        if c == 2 and output:
                            pe.wait_ge(s_v, cnt(s_v, pr * 2 + (2 if scores else 0)))
                            if soft and softmax:
                                pe.wait_ge(s_neg, cnt(s_neg, u))
                            project_out(u - 3)
                    if isinstance(k, int) and k == 1:
                        pe.wait_ge(s_wo_in, (e + 1) * (16 * wo_dma))
                        if bias is not None:
                            pe.wait_ge(s_neg, cnt(s_neg, u))
                            fold_bias(e)
                    for c in range(1, SETS):
                        if soft:
                            score_t(u - 1, c, (j - 1) % 4)

                steps(pe, slot, first)

            @block.scalar
            def _(act):
                act.wait_ge(s_init, INIT)
                def take_qk(pr):
                    act.wait_ge(s_qk, pr + 1)
                    act.wait_ge(s_qlo, cnt(s_qlo, pr))
                    act.wait_ge(s_klo, cnt(s_klo, pr))
                    for dst, src, b in ((q_full, ps_qk[:, 0:2 * S], 0), (k_full, ps_qk[:, 256:256 + 2 * NK], 1)):
                        if bias is not None:
                            ins = act.activation(dst[:, :], src, ACT.Identity, bias=(b_q, b_k)[b][:, 0:1])
                        else:
                            ins = act.activation(dst[:, :], src, ACT.Copy)
                        ins.then_inc(s_qke, 1)

                def take_v(pr, par):
                    act.wait_ge(s_pv, cnt(s_pv, pr + 1))
                    act.wait_ge(s_av, cnt(s_av, pr * 2 - 2))
                    for i in range(2):
                        src = ps_v[0:NK, i * D:(i + 1) * D].rearrange("p (t s d) -> p t s d", t=SETS, s=4)
                        dst = strided(vpad[par][i][:, :, :, :], 0, [[512, NK], [136, SETS], [32, 4], [1, HD]])
                        act.activation(dst, src, ACT.Copy).then_inc(s_v, 1)

                def exponents(u, c, j):
                    i = j % 2
                    act.wait_ge(s_st, cnt(s_st, u * 4 + c + 1))
                    if c == 0:
                        act.wait_ge(s_av, cnt(s_av, u - 1))
                    act.activation(probs[i][0:NK, c, :], ps_st[c % 3][0:NK, :], ACT.Sigmoid if sigmoid else ACT.Exp,
                                   scale=scale).then_inc(s_prob, 1)

                def take_o(u):
                    act.wait_ge(s_av, cnt(s_av, u + 1))
                    done = s_norm if softmax else s_out
                    act.wait_ge(done, cnt(done, u))
                    if softmax:
                        take_sums(u)
                    act.activation(o_sb[:, :], ps_o[:, 0:2 * S], ACT.Copy).then_inc(s_o, 1)

                def take_sums(u):
                    act.wait_ge(s_rec, cnt(s_rec, u))
                    act.activation(sums[:, :], ps_o[:, 0:S], ACT.Identity, bias=is_sum[:, 1:2],
                                   scale=is_sum[:, 0:1]).then_inc(s_sumc, 1)

                def first(e):
                    take_qk(e * PAIRS)
                    take_qk(e * PAIRS + 1)

                def place_maxima(u, j):
                    act.wait_ge(s_neg, cnt(s_neg, u + 1))
                    if mask is None:
                        dst = qbd[j // 2][MAXROW:MAXROW + 1, :, :, j % 2, :].rearrange("p t s q -> p (t s) q")
                    else:
                        dst = maxrow[j % 2][:, :, :]
                    act.dma_start(dst, negmax[:, :]).then_inc(s_negd, 16)

                def slot(u, pr, kp, k, j, scores, soft, values, output, next_pair, e):
                    i = j % 2
                    if soft and softmax:
                        place_maxima(u - 1, (j - 1) % 4)
                    if i == 0 and scores:
                        take_v(pr, j // 2)
                    if i == 1 and next_pair == 2:
                        take_qk(pr + 2)
                    for c in range(SETS):
                        if soft:
                            exponents(u - 1, c, j - 1)
                        if c == 0 and values:
                            take_o(u - 2)

                steps(act, slot, first)

            @block.vector
            def _(dve):
                if softmax:
                    dve.memset(sum_last[:, :], 0.0).then_inc(s_pad, 1)
                    dve.wait_ge(s_pad, 1)
                    dve.memset(sum_last[:, 27:28], 1.0).then_inc(s_pad, 1)
                dve.wait_ge(s_init, INIT)
                for i in range(2):
                    for jj in range(2):
                        if softmax:
                            dve.memset(strided(vpad[i][jj][:, :, :, :], 24, [[512, P], [129, 3], [32, 4]]), 1.0).then_inc(s_pad, 1)
                            dve.memset(strided(vpad[i][jj][:, :, :, :], 384, [[512, P], [32, 4]]), 1.0).then_inc(s_pad, 1)
                if mask is not None:
                    dve.tensor_scalar(maskneg[:, :], maskraw[:, :], 0.0, MASKED, ALU.is_equal, ALU.mult).then_inc(s_mask, 1)

                def maxima(u, c, j):
                    dve.wait_ge(s_score, u * 4 + c + 1)
                    if c == 0:
                        dve.wait_ge(s_mt, cnt(s_mt, u - 1))
                    dve.tensor_reduce(rowmax[j % 2][:, 4 * c:4 * c + 4],
                                      ps_s[c % 2][:, 0:4 * NK].rearrange("p (s k) -> p s k", s=4), AX.X,
                                      ALU.max).then_inc(s_max, 1)

                def negate(u):
                    dve.wait_ge(s_mt, cnt(s_mt, u + 1))
                    dve.wait_ge(s_negd, cnt(s_negd, u * 16))
                    dve.tensor_scalar(negmax[:, :], ps_mt, -1.0, None, ALU.mult).then_inc(s_neg, 1)

                def invert(u):
                    dve.wait_ge(s_sumc, cnt(s_sumc, u + 1))
                    dve.wait_ge(s_sum, u)
                    dve.reciprocal(recip[:, :], sums[:, :]).then_inc(s_rec, 1)

                def normalise(u):
                    dve.wait_ge(s_sum, u + 1)
                    dve.wait_ge(s_o, cnt(s_o, u + 1))
                    dve.wait_ge(s_out, cnt(s_out, u))
                    dve.tensor_tensor(o_norm[:, :], o_sb[:, :], ps_sum[:, 0:2 * S], ALU.mult).then_inc(s_norm, 1)

                def update(u, k, e):
                    dve.wait_ge(s_out, cnt(s_out, u + 1))
                    xb = x[:, k, :]
                    by = gate[:, bass.ds(k * experts + e, 1)] if gate is not None else coef
                    dve.scalar_tensor_tensor(xb, ps_out, by, xb, ALU.mult, ALU.add).then_inc(s_upd, 1)

                def first(e):
                    pass

                def slot(u, pr, kp, k, j, scores, soft, values, output, next_pair, e):
                    par, i = j // 2, j % 2
                    if soft and softmax:
                        negate(u - 1)
                    for c in range(SETS):
                        if scores and softmax:
                            maxima(u, c, j)
                        if c == 1 and output and softmax:
                            normalise(u - 3)
                        if c == 3 and output:
                            update(u - 3, k - 3, e)
                    if values and softmax:
                        invert(u - 2)
                    if bias is not None and isinstance(k, int) and k == 1:
                        dve.wait_ge(s_fold, e + 1)
                        dve.tensor_tensor(w_o[0:1, 1, :], w_o[0:1, 1, :], ps_out[0:1, :], ALU.add).then_inc(s_wo, 1)

                steps(dve, slot, first)
                dve.wait_ge(s_upd, cnt(s_upd, experts * U))


def skewed(eng, n, depth, unroll, slot):
    lead = -(-depth // unroll) * unroll
    for i in range(lead):
        slot(i, i % unroll, lambda d, i=i: 0 <= i - d < n)
    with eng.Fori(lead // unroll, n // unroll) as it:
        for j in range(unroll):
            slot(it * unroll + j, j, lambda d: True)
    for i in range(n, n + depth):
        slot(i, i % unroll, lambda d, i=i: i - d < n)


class Signal:

    def __init__(self, core, name, ctx, ahead=0):
        self.sem, self.ahead = core.sem(name, ctx), ahead

    def after(self, steps):
        return steps + self.ahead


def start_ahead(eng, signals):
    for s in signals:
        if s.ahead:
            eng.sem_inc(s.sem, s.ahead)


def project_tokens(nc, core, name, srcT, w, M, dst, bias=None):
    GB = 4
    steps = B // GB
    with ExitStack() as ctx:
        w_sb = core.sb("w_sb", [P, P], ctx=ctx)
        b_sb = core.sb("b_sb", [P, 1], ctx=ctx)
        rows = [core.sb(f"rows{i}", [P, GB * S], ctx=ctx) for i in range(2)]
        ps_r = [core.ps(f"ps_r{i}", [P, GB * S], ctx) for i in range(2)]
        ps_t = [core.ps(f"ps_t{i}", [P, GB * P], ctx) for i in range(2)]
        s_w = core.sem(f"{name}_w", ctx)
        s_mm, s_rows, s_tr, s_out = (Signal(core, f"{name}_{n}", ctx, a) for n, a in
                                     (("mm", 0), ("rows", 2), ("tr", 2), ("out", 2)))
        with nc.Block() as block:

            @block.sync
            def _(sp):
                start_ahead(sp, (s_rows, s_tr, s_out))
                sp.dma_start(w_sb[:, :], w).then_inc(s_w, 16)
                if bias is not None:
                    sp.dma_start(b_sb[:, :], bias).then_inc(s_w, 16)
                sp.wait_ge(s_w, 32 if bias is not None else 16)

            @block.tensor
            def _(pe):
                pe.wait_ge(s_w, 16 if bias is None else 32)

                def slot(i, j, live):
                    if live(0):
                        pe.wait_ge(s_rows.sem, s_rows.after(i - 1))
                        pe.matmul(ps_r[j][:, :], w_sb[:, :], srcT[:, bass.ds(i * (GB * S), GB * S)], start=True,
                                  stop=True).then_inc(s_mm.sem, 1)
                    if live(1):
                        pe.wait_ge(s_rows.sem, s_rows.after(i))
                        pe.wait_ge(s_out.sem, s_out.after(i - 2))
                        for b in range(GB):
                            mm = pe.transpose(ps_t[1 - j][:, b * P:(b + 1) * P], rows[1 - j][:, b * S:(b + 1) * S],
                                              core.ident[:, :])
                        mm.then_inc(s_tr.sem, 1)
                skewed(pe, steps, 1, 2, slot)

            @block.scalar
            def _(act):
                act.wait_ge(s_w, 16 if bias is None else 32)

                def slot(i, j, live):
                    act.wait_ge(s_mm.sem, i + 1)
                    act.wait_ge(s_tr.sem, s_tr.after(i - 1))
                    if bias is not None:
                        ins = act.activation(rows[j][:, :], ps_r[j][:, :], ACT.Identity, bias=b_sb[:, 0:1])
                    else:
                        ins = act.activation(rows[j][:, :], ps_r[j][:, :], ACT.Copy)
                    ins.then_inc(s_rows.sem, 1)
                skewed(act, steps, 0, 2, slot)

            @block.vector
            def _(dve):
                def slot(i, j, live):
                    dve.wait_ge(s_tr.sem, s_tr.after(i + 1))
                    dve.tensor_copy(dst[:, bass.ds(i * GB, GB), :],
                                    ps_t[j][:, :].rearrange("p (b m) -> p b m", b=GB)[:, :, 0:M]).then_inc(s_out.sem, 1)
                skewed(dve, steps, 0, 2, slot)
                dve.wait_ge(s_out.sem, s_out.after(steps))


def transpose_tokens(nc, core, name, src, dstT):
    GB = 4
    steps = B // GB
    with ExitStack() as ctx:
        tile = [core.sb(f"tile{i}", [P, GB, P], ctx=ctx) for i in range(2)]
        ps_t = [core.ps(f"ps_t{i}", [P, GB * S], ctx) for i in range(2)]
        s_in, s_tr, s_out = (Signal(core, f"{name}_{n}", ctx, a) for n, a in (("in", 0), ("tr", 2), ("out", 2)))
        with nc.Block() as block:

            @block.sync
            def _(sp):
                start_ahead(sp, (s_tr, s_out))

            @block.vector
            def _(dve):
                def slot(i, j, live):
                    dve.wait_ge(s_tr.sem, s_tr.after(i - 1))
                    dve.tensor_copy(tile[j][:, :, :], src[:, bass.ds(i * GB, GB), :]).then_inc(s_in.sem, 1)
                skewed(dve, steps, 0, 2, slot)

            @block.tensor
            def _(pe):
                def slot(i, j, live):
                    pe.wait_ge(s_in.sem, i + 1)
                    pe.wait_ge(s_out.sem, s_out.after(i - 1))
                    for b in range(GB):
                        mm = pe.transpose(ps_t[j][:, b * S:(b + 1) * S], tile[j][:, b, :], core.ident[:, :])
                    mm.then_inc(s_tr.sem, 1)
                skewed(pe, steps, 0, 2, slot)

            @block.scalar
            def _(act):
                def slot(i, j, live):
                    act.wait_ge(s_tr.sem, s_tr.after(i + 1))
                    act.activation(dstT[:, bass.ds(i * (GB * S), GB * S)], ps_t[j][:, :], ACT.Copy).then_inc(s_out.sem, 1)
                skewed(act, steps, 0, 2, slot)
                act.wait_ge(s_out.sem, s_out.after(steps))


def top_two(nc, core, name, logits, E, oh, w, rank=None):
    with ExitStack() as ctx:
        desc_i = core.sb("desc_i", [P, E], mybir.dt.int32, ctx)
        desc = core.sb("desc", [P, E], ctx=ctx)
        top = [core.sb(f"top{i}", [P, B], ctx=ctx) for i in range(2)]
        rk = rank or [core.sb(f"rk{i}", [P, B], ctx=ctx) for i in range(2)]
        tmp = core.sb("tmp", [P, B, E], ctx=ctx)
        ex = core.sb("ex", [P, B], ctx=ctx)
        s_desc, s_step, s_exp = (core.sem(f"{name}_{n}", ctx) for n in ("desc", "step", "exp"))

        def wide(v):
            return v[:, :].unsqueeze(2).to_broadcast([P, B, E])
        with nc.Block() as block:

            @block.gpsimd
            def _(pool):
                pool.iota(desc_i[:, :], [[-1, E]], base=E, channel_multiplier=0).then_inc(s_desc, 1)
                pool.wait_ge(s_desc, 1)
                pool.tensor_copy(desc[:, :], desc_i[:, :]).then_inc(s_desc, 1)
                pool.wait_ge(s_desc, 2)

            @block.vector
            def _(dve):
                done = [0]

                def step(ins):
                    done[0] += 1
                    ins.then_inc(s_step, 1)
                    dve.wait_ge(s_step, done[0])

                dve.wait_ge(s_desc, 2)
                dvec = desc[:, :].unsqueeze(1).to_broadcast([P, B, E])
                for i in range(2):
                    step(dve.tensor_reduce(top[i][:, :], logits[:, :, :], AX.X, ALU.max))
                    step(dve.tensor_tensor(tmp[:, :, :], logits[:, :, :], wide(top[i]), ALU.is_equal))
                    step(dve.tensor_tensor(tmp[:, :, :], tmp[:, :, :], dvec, ALU.mult))
                    step(dve.tensor_reduce(rk[i][:, :], tmp[:, :, :], AX.X, ALU.max))
                    step(dve.tensor_tensor(oh[i][:, :, :], tmp[:, :, :], wide(rk[i]), ALU.is_equal))
                    if i == 0:
                        step(dve.scalar_tensor_tensor(logits[:, :, :], oh[0][:, :, :], -1e30, logits[:, :, :],
                                                      ALU.mult, ALU.add))
                step(dve.tensor_tensor(top[1][:, :], top[1][:, :], top[0][:, :], ALU.subtract))
                dve.wait_ge(s_exp, 1)
                step(dve.tensor_scalar(top[0][:, :], ex[:, :], 1.0, None, ALU.add))
                step(dve.reciprocal(w[0][:, :], top[0][:, :]))
                step(dve.tensor_tensor(w[1][:, :], ex[:, :], w[0][:, :], ALU.mult))

            @block.scalar
            def _(act):
                act.wait_ge(s_step, 12)
                act.activation(ex[:, :], top[1][:, :], ACT.Exp).then_inc(s_exp, 1)


def layer0_gates(nc, core, inp, gate):
    H = D // 2
    with ExitStack() as ctx:
        h = core.sb("h", [P, B, P], ctx=ctx)
        project_tokens(nc, core, "r0a", core.xnT, inp["r0_w1"], P, h, inp["r0_b1"])
        with ExitStack() as ictx:
            stats = core.sb("r0stats", [P, B, 6], ctx=ictx)
            tmp = [core.sb(f"r0tmp{i}", [P, B], ctx=ictx) for i in range(3)]
            mhalf = core.sb("r0mhalf", [P, B], ctx=ictx)
            rstd = core.sb("r0rstd", [P, B], ctx=ictx)
            ln_g, ln_b = core.sb("ln_g", [P, H], ctx=ictx), core.sb("ln_b", [P, H], ctx=ictx)
            s_c, s_st, s_step, s_pow = (core.sem(f"r0n_{n}", ictx) for n in ("c", "st", "step", "pow"))
            with nc.Block() as block:

                @block.sync
                def _(sp):
                    sp.dma_start(ln_g[:, :], inp["ln_g"].partition_broadcast(P)).then_inc(s_c, 16)
                    sp.dma_start(ln_b[:, :], inp["ln_b"].partition_broadcast(P)).then_inc(s_c, 16)
                    sp.wait_ge(s_c, 32)

                @block.gpsimd
                def _(pool):
                    pool.memset(mhalf[:, :], -0.5).then_inc(s_pow, 1)
                    pool.wait_ge(s_pow, 1)
                    pool.wait_ge(s_step, 7)
                    pool.tensor_tensor(rstd[:, :], tmp[0][:, :], mhalf[:, :], ALU.pow).then_inc(s_pow, 1)

                @block.vector
                def _(dve):
                    done = [0]

                    def step(ins):
                        done[0] += 1
                        ins.then_inc(s_step, 1)
                        dve.wait_ge(s_step, done[0])

                    with dve.Fori(0, B // 4) as it:
                        for j in range(4):
                            dve.bn_stats(stats[:, it * 4 + j, :], h[:, it * 4 + j, 0:H]).then_inc(s_st, 1)
                    dve.wait_ge(s_st, B)
                    me, mo = stats[:, :, 1], stats[:, :, 4]
                    step(dve.tensor_tensor(tmp[0][:, :], me, mo, ALU.add))
                    step(dve.tensor_tensor(tmp[1][:, :], me, mo, ALU.subtract))
                    step(dve.tensor_tensor(tmp[2][:, :], stats[:, :, 2], stats[:, :, 5], ALU.add))
                    step(dve.scalar_tensor_tensor(tmp[1][:, :], tmp[1][:, :], 0.25, tmp[1][:, :], ALU.mult, ALU.mult))
                    step(dve.tensor_scalar(tmp[2][:, :], tmp[2][:, :], 1.0 / H, EPS, ALU.mult, ALU.add))
                    step(dve.tensor_scalar(stats[:, :, 0], tmp[0][:, :], 0.5, None, ALU.mult))
                    step(dve.tensor_tensor(tmp[0][:, :], tmp[1][:, :], tmp[2][:, :], ALU.add))
                    hv = h[:, :, 0:H]

                    def per_b(v):
                        return v.unsqueeze(2).to_broadcast([P, B, H])

                    def per_h(v):
                        return v[:, :].unsqueeze(1).to_broadcast([P, B, H])
                    step(dve.tensor_tensor(hv, hv, per_b(stats[:, :, 0]), ALU.subtract))
                    dve.wait_ge(s_pow, 2)
                    step(dve.tensor_tensor(hv, hv, per_b(rstd[:, :]), ALU.mult))
                    dve.wait_ge(s_c, 32)
                    step(dve.tensor_tensor(hv, hv, per_h(ln_g), ALU.mult))
                    step(dve.tensor_tensor(hv, hv, per_h(ln_b), ALU.add))
                    step(dve.tensor_scalar(hv, hv, 0.0, None, ALU.max))
        with ExitStack() as ictx:
            hT = core.sb("hT", [P, B * S], ctx=ictx)
            logits = core.sb("logits", [P, B, E0], ctx=ictx)
            oh = [core.sb(f"oh{i}", [P, B, E0], ctx=ictx) for i in range(2)]
            w = [core.sb(f"w{i}", [P, B], ctx=ictx) for i in range(2)]
            transpose_tokens(nc, core, "r0t", h, hT)
            project_tokens(nc, core, "r0b", hT, inp["r0_w2"], E0, logits, inp["r0_b2"])
            top_two(nc, core, "r0k", logits, E0, oh, w)
            combine_gates(nc, core, "r0g", oh, w, E0, core.tanh_g[:, 4:5], gate)


def combine_gates(nc, core, name, oh, w, E, g, gate):
    with ExitStack() as ctx:
        s_step = core.sem(f"{name}_step", ctx)
        with nc.Block() as block:

            @block.vector
            def _(dve):
                for i in range(2):
                    dve.scalar_tensor_tensor(oh[i][:, :, :], oh[i][:, :, :], g,
                                             w[i][:, :].unsqueeze(2).to_broadcast([P, B, E]), ALU.mult,
                                             ALU.mult).then_inc(s_step, 1)
                dve.wait_ge(s_step, 2)
                dve.tensor_tensor(gate[:, :].rearrange("p (b e) -> p b e", e=E), oh[0][:, :, :], oh[1][:, :, :],
                                  ALU.add).then_inc(s_step, 1)
                dve.wait_ge(s_step, 3)


def context_attention(nc, core, name, w_out, scale, coef, mix=None):
    GB = 4
    steps = B // GB
    with ExitStack() as ctx:
        query = [core.sb(f"{name}_query{i}", [P, GB * S], ctx=ctx) for i in range(2)]
        values = [core.sb(f"{name}_values{i}", [NC, GB, D], ctx=ctx) for i in range(4)]
        probs = [core.sb(f"{name}_probs{i}", [P, GB, P], ctx=ctx) for i in range(2)]
        probsT = [core.sb(f"{name}_probsT{i}", [P, GB * S], ctx=ctx) for i in range(2)]
        attT = [core.sb(f"{name}_attT{i}", [P, GB * S], ctx=ctx) for i in range(2)]
        bias_m = [core.sb(f"{name}_bias_m{i}", [P, GB], ctx=ctx) for i in range(2)]
        sums = [core.sb(f"{name}_sums{i}", [P, GB], ctx=ctx) for i in range(2)]
        recip = [core.sb(f"{name}_recip{i}", [P, GB], ctx=ctx) for i in range(2)]
        by = [core.sb(f"{name}_by{i}", [P, GB], ctx=ctx) for i in range(4)]
        if mix is None:
            w_o = core.sb(f"{name}_w_o", [P, D], ctx=ctx)
        else:
            w_sim = core.sb(f"{name}_w_sim", [P, 2], ctx=ctx)
            w4 = core.sb(f"{name}_w4", [P, 4, D], ctx=ctx)
            w_first = [core.sb(f"{name}_w_first{i}", [P, GB, D], ctx=ctx) for i in range(2)]
            xs = [core.sb(f"{name}_xs{i}", [P, GB * S], ctx=ctx) for i in range(2)]
            xa = [core.sb(f"{name}_xa{i}", [P, GB * S], ctx=ctx) for i in range(2)]
            bias = core.sb(f"{name}_bias", [P, D], ctx=ctx)
        ps_s, ps_t, ps_a, ps_o = ([core.ps(f"{name}_{n}{i}", [P, 512], ctx) for i in range(2)]
                                  for n in ("ps_s", "ps_t", "ps_a", "ps_o"))
        s_w, s_small, s_zero = (core.sem(f"{name}_{n}", ctx) for n in ("w", "small", "zero"))
        s_val = [core.sem(f"{name}_val{i}", ctx) for i in range(4)]
        s_query, s_score, s_max, s_exp, s_rec, s_pn, s_tr, s_pt, s_av, s_at, s_out, s_upd = (
            Signal(core, f"{name}_{n}", ctx, 4) for n in
            ("query", "score", "max", "exp", "rec", "pn", "tr", "pt", "av", "at", "out", "upd"))
        s_xs, s_wf, s_xa = (Signal(core, f"{name}_{n}", ctx, 4) for n in ("xs", "wf", "xa"))
        wdma = 16 * (1 if mix is None else 3)

        with nc.Block() as block:

            @block.sync
            def _(sp):
                start_ahead(sp, (s_query, s_score, s_max, s_exp, s_rec, s_pn, s_tr, s_pt, s_av, s_at, s_out, s_upd,
                                 s_xs, s_wf, s_xa))
                if mix is None:
                    sp.dma_start(w_o[:, :], w_out).then_inc(s_w, 16)
                else:
                    sp.dma_start(w_sim[:, :], mix[0]).then_inc(s_w, 16)
                    sp.dma_start(w4[:, :, :], mix[1]).then_inc(s_w, 16)
                    sp.dma_start(bias[:, :], mix[3].partition_broadcast(P)).then_inc(s_w, 16)

                def slot(i, j, live):
                    if live(0):
                        sp.wait_ge(s_av.sem, s_av.after(i - 3))
                        sp.dma_start(values[j][:, :, :], core.inp["ctx_1024"][bass.ds(i * GB, GB), :, :]
                                     .rearrange("b s d -> s b d")).then_inc(s_val[j], 16)
                skewed(sp, steps, 0, 4, slot)
                sp.wait_ge(s_w, wdma)

            @block.gpsimd
            def _(pool):
                for i in range(2):
                    pool.memset(probs[i][:, :, :], 0.0).then_inc(s_zero, 1)
                pool.wait_ge(s_zero, 2)

                def slot(i, j, live):
                    if live(2):
                        pool.wait_ge(s_out.sem, s_out.after(i - 3))
                        pool.tensor_tensor(xs[j % 2][:, :], core.xnT[:, bass.ds(i * (GB * S) - 2 * GB * S, GB * S)],
                                           probs_zero(), ALU.add).then_inc(s_xs.sem, 1)

                def probs_zero():
                    return strided(probs[0][:, :, :], NC, [[GB * P, P], [0, GB * S // 8], [1, 8]])
                if mix is not None:
                    skewed(pool, steps, 2, 4, slot)

            @block.scalar
            def _(act):
                act.wait_ge(s_w, wdma)
                act.wait_ge(s_zero, 2)

                def slot(i, j, live):
                    p = j % 2
                    if live(0):
                        act.wait_ge(s_score.sem, s_score.after(i - 1))
                        src = core.xnT[:, bass.ds(i * (GB * S), GB * S)]
                        if mix is None:
                            ins = act.activation(query[p][:, :], src, ACT.Copy)
                        else:
                            ins = act.activation(query[p][:, :], src, ACT.Identity, bias=w_sim[:, 1:2],
                                                 scale=w_sim[:, 0:1])
                        ins.then_inc(s_query.sem, 1)
                    if live(2):
                        act.wait_ge(s_tr.sem, s_tr.after(i - 1))
                        act.wait_ge(s_av.sem, s_av.after(i - 3))
                        act.activation(probsT[p][:, :], ps_t[p][:, :], ACT.Copy).then_inc(s_pt.sem, 1)
                    if live(1):
                        act.wait_ge(s_max.sem, s_max.after(i))
                        act.wait_ge(s_tr.sem, s_tr.after(i - 2))
                        act.wait_ge(s_rec.sem, s_rec.after(i - 2))
                        for b in range(GB):
                            ins = act.activation(probs[1 - p][:, b, 0:NC], ps_s[1 - p][:, b * NC:(b + 1) * NC], ACT.Exp,
                                                 bias=bias_m[1 - p][:, b:b + 1], scale=scale,
                                                 accum_out=sums[1 - p][:, b:b + 1])
                        ins.then_inc(s_exp.sem, 1)
                    if live(2) and mix is not None:
                        act.wait_ge(s_av.sem, s_av.after(i - 1))
                        act.wait_ge(s_out.sem, s_out.after(i - 3))
                        act.wait_ge(s_xa.sem, s_xa.after(i - 3))
                        act.activation(attT[p][:, :], ps_a[p][:, :], ACT.Copy).then_inc(s_at.sem, 1)
                skewed(act, steps, 2, 4, slot)

            @block.tensor
            def _(pe):
                pe.wait_ge(s_w, wdma)

                def slot(i, j, live):
                    p = j % 2
                    if live(0):
                        pe.wait_ge(s_query.sem, s_query.after(i + 1))
                        pe.wait_ge(s_exp.sem, s_exp.after(i - 1))
                        for b in range(GB):
                            mm = pe.matmul(ps_s[p][:, b * NC:(b + 1) * NC], query[p][:, b * S:(b + 1) * S],
                                           core.ctxT[:, bass.ds(i * (GB * NC) + b * NC, NC)], start=True, stop=True)
                        mm.then_inc(s_score.sem, 1)
                    if live(3):
                        pe.wait_ge(s_at.sem, s_at.after(i - 2))
                        pe.wait_ge(s_upd.sem, s_upd.after(i - 4))
                        if mix is not None:
                            pe.wait_ge(s_xs.sem, s_xs.after(i - 2))
                            pe.wait_ge(s_wf.sem, s_wf.after(i - 2))
                            pe.wait_ge(s_xa.sem, s_xa.after(i - 2))
                        for b in range(GB):
                            out = ps_o[1 - p][:, b * D:(b + 1) * D]
                            cols = slice(b * S, (b + 1) * S)
                            if mix is None:
                                mm = pe.matmul(out, attT[1 - p][:, cols], w_o[:, :], start=True, stop=True)
                            else:
                                pe.matmul(out, xs[1 - p][:, cols], w_first[1 - p][:, b, :], start=True, stop=False)
                                pe.matmul(out, attT[1 - p][:, cols], w4[:, 1, :], start=False, stop=False)
                                mm = pe.matmul(out, xa[1 - p][:, cols], w4[:, 2, :], start=False, stop=True)
                        mm.then_inc(s_out.sem, 1)
                    if live(2):
                        pe.wait_ge(s_pt.sem, s_pt.after(i - 1))
                        pe.wait_ge(s_at.sem, s_at.after(i - 3))
                        pe.wait_ge(s_val[(j - 2) % 4], (i - 2 - (j - 2) % 4) * 4 + 16)
                        for b in range(GB):
                            mm = pe.matmul(ps_a[p][:, b * S:(b + 1) * S], values[(j - 2) % 4][:, b, :],
                                           probsT[p][0:NC, b * S:(b + 1) * S], start=True, stop=True)
                        mm.then_inc(s_av.sem, 1)
                    if live(1):
                        ready = s_exp if mix is None else s_pn
                        pe.wait_ge(ready.sem, ready.after(i))
                        pe.wait_ge(s_pt.sem, s_pt.after(i - 2))
                        for b in range(GB):
                            mm = pe.transpose(ps_t[1 - p][:, b * S:(b + 1) * S], probs[1 - p][:, b, :],
                                              core.ident[:, :])
                        mm.then_inc(s_tr.sem, 1)
                skewed(pe, steps, 3, 4, slot)

            @block.vector
            def _(dve):
                dve.wait_ge(s_w, wdma)

                def slot(i, j, live):
                    p = j % 2
                    if live(0):
                        dve.wait_ge(s_score.sem, s_score.after(i + 1))
                        dve.wait_ge(s_exp.sem, s_exp.after(i - 1))
                        dve.tensor_reduce(bias_m[p][:, :], ps_s[p][:, 0:GB * NC].rearrange("p (b k) -> p b k", b=GB),
                                          AX.X, ALU.max).then_inc(s_small, 1)
                        dve.wait_ge(s_small, i + 1)
                        dve.tensor_scalar(bias_m[p][:, :], bias_m[p][:, :], -scale, None, ALU.mult
                                          ).then_inc(s_max.sem, 1)
                    if live(1):
                        dve.wait_ge(s_exp.sem, s_exp.after(i))
                        dve.reciprocal(recip[1 - p][:, :], sums[1 - p][:, :]).then_inc(s_rec.sem, 1)
                        dve.wait_ge(s_rec.sem, s_rec.after(i))
                        if mix is None:
                            dve.wait_ge(s_upd.sem, s_upd.after(i - 4))
                            dve.tensor_scalar(by[(j - 1) % 4][:, :], recip[1 - p][:, :], coef, None, ALU.mult
                                              ).then_inc(s_pn.sem, 1)
                        else:
                            dve.tensor_tensor(probs[1 - p][:, :, 0:NC], probs[1 - p][:, :, 0:NC],
                                              recip[1 - p][:, :].unsqueeze(2).to_broadcast([P, GB, NC]), ALU.mult
                                              ).then_inc(s_pn.sem, 1)
                    if live(2) and mix is None:
                        dve.wait_ge(s_av.sem, s_av.after(i - 1))
                        dve.wait_ge(s_out.sem, s_out.after(i - 3))
                        dve.tensor_copy(attT[p][:, :], ps_a[p][:, :]).then_inc(s_at.sem, 1)
                    if live(3):
                        dve.wait_ge(s_out.sem, s_out.after(i - 2))
                        if mix is None:
                            dve.wait_ge(s_pn.sem, s_pn.after(i - 2))
                        for b in range(GB):
                            xb = core.x[:, bass.ds(i * GB + (b - 3 * GB), 1), :]
                            ins = dve.scalar_tensor_tensor(xb, ps_o[1 - p][:, b * D:(b + 1) * D].unsqueeze(1),
                                                           by[(j - 3) % 4][:, b:b + 1] if mix is None else coef, xb,
                                                           ALU.mult, ALU.add)
                        ins.then_inc(s_upd.sem, 1)
                    if live(2) and mix is not None:
                        dve.wait_ge(s_out.sem, s_out.after(i - 3))
                        for b in range(GB):
                            ins = dve.scalar_tensor_tensor(w_first[p][:, b, :], w4[:, 3, :],
                                                           mix[2][:, bass.ds(i * GB + (b - 2 * GB), 1)], w4[:, 0, :],
                                                           ALU.mult, ALU.add)
                        ins.then_inc(s_wf.sem, 1)
                        dve.wait_ge(s_at.sem, s_at.after(i - 1))
                        dve.tensor_tensor(xa[p][:, :], attT[p][:, :],
                                          core.xnT[:, bass.ds(i * (GB * S) - 2 * GB * S, GB * S)], ALU.mult
                                          ).then_inc(s_xa.sem, 1)
                skewed(dve, steps, 3, 4, slot)
                dve.wait_ge(s_upd.sem, s_upd.after(steps))
                if mix is not None:
                    dve.tensor_scalar(bias[:, :], bias[:, :], coef, None, ALU.mult).then_inc(s_upd.sem, 1)
                    dve.wait_ge(s_upd.sem, s_upd.after(steps + 1))
                    dve.tensor_tensor(core.x[:, :, :], core.x[:, :, :],
                                      bias[:, :].unsqueeze(1).to_broadcast([P, B, D]), ALU.add).then_inc(s_upd.sem, 1)
                    dve.wait_ge(s_upd.sem, s_upd.after(steps + 2))


def best_token_context(nc, core, name, w_sim, w1, b_sim, hc):
    GB = 4
    steps = B // GB
    with ExitStack() as ctx:
        own = core.sb("own", [P, B, 1], ctx=ctx)
        best = core.sb("best", [P, P], ctx=ctx)
        wide = nc.dram_tensor(f"{name}_wide", (B, S), F32, kind="Internal").ap()
        project_tokens(nc, core, f"{name}p", core.xnT, w1, 1, own, b_sim)
        with ExitStack() as ictx:
            w = core.sb("w", [P, 2], ctx=ictx)
            query = [core.sb(f"query{i}", [P, GB * S], ctx=ictx) for i in range(2)]
            ps_s = [core.ps(f"ps_s{i}", [P, 512], ictx) for i in range(2)]
            ps_b = core.ps("ps_b", [P, 512], ictx)
            top, total, weight = (core.sb(n, [P, 1], ctx=ictx) for n in ("top", "total", "weight"))
            spreadw = core.sb("spreadw", [P, S], ctx=ictx)
            s_w, s_zero, s_tr, s_step, s_store = (core.sem(f"{name}_{n}", ictx) for n in
                                                  ("w", "zero", "tr", "step", "store"))
            s_query, s_score, s_best = (Signal(core, f"{name}_{n}", ictx, 2) for n in ("query", "score", "best"))
            with nc.Block() as block:

                @block.sync
                def _(sp):
                    start_ahead(sp, (s_query, s_score, s_best))
                    sp.dma_start(w[:, :], w_sim).then_inc(s_w, 16)
                    sp.wait_ge(s_w, 16)
                    sp.wait_ge(s_step, 5)
                    sp.dma_start(wide, spreadw[0:B, :]).then_inc(s_store, 16)
                    sp.wait_ge(s_store, 16)

                @block.gpsimd
                def _(pool):
                    pool.memset(best[:, :], 0.0).then_inc(s_zero, 1)
                    pool.wait_ge(s_zero, 1)

                @block.scalar
                def _(act):
                    act.wait_ge(s_w, 16)

                    def slot(i, j, live):
                        act.wait_ge(s_score.sem, s_score.after(i - 1))
                        act.activation(query[j][:, :], core.xnT[:, bass.ds(i * (GB * S), GB * S)], ACT.Identity,
                                       bias=w[:, 1:2], scale=w[:, 0:1]).then_inc(s_query.sem, 1)
                    skewed(act, steps, 0, 2, slot)
                    act.wait_ge(s_step, 2)
                    act.activation(spreadw[:, :], ps_b[:, 0:S], ACT.Exp, bias=top[:, 0:1],
                                   accum_out=total[:, 0:1]).then_inc(s_step, 1)

                @block.tensor
                def _(pe):
                    def slot(i, j, live):
                        pe.wait_ge(s_query.sem, s_query.after(i + 1))
                        pe.wait_ge(s_best.sem, s_best.after(i - 1))
                        for b in range(GB):
                            mm = pe.matmul(ps_s[j][:, b * NC:(b + 1) * NC], query[j][:, b * S:(b + 1) * S],
                                           core.ctxT[:, bass.ds(i * (GB * NC) + b * NC, NC)], start=True, stop=True)
                        mm.then_inc(s_score.sem, 1)
                    skewed(pe, steps, 0, 2, slot)
                    pe.wait_ge(s_tr, 1)
                    pe.transpose(ps_b[:, 0:S], best[:, :], core.ident[:, :]).then_inc(s_tr, 1)

                @block.vector
                def _(dve):
                    dve.wait_ge(s_zero, 1)

                    def slot(i, j, live):
                        dve.wait_ge(s_score.sem, s_score.after(i + 1))
                        dve.tensor_reduce(best[:, bass.ds(i * GB, GB)],
                                          ps_s[j][:, 0:GB * NC].rearrange("p (b k) -> p b k", b=GB), AX.X,
                                          ALU.max).then_inc(s_best.sem, 1)
                    skewed(dve, steps, 0, 2, slot)
                    dve.wait_ge(s_best.sem, s_best.after(steps))
                    dve.tensor_tensor(best[:, 0:B], best[:, 0:B], own[:, :, 0], ALU.add).then_inc(s_tr, 1)
                    dve.wait_ge(s_tr, 2)
                    dve.tensor_reduce(top[:, :], ps_b[:, 0:S], AX.X, ALU.max).then_inc(s_step, 1)
                    dve.wait_ge(s_step, 1)
                    dve.tensor_scalar(top[:, :], top[:, :], -1.0, None, ALU.mult).then_inc(s_step, 1)
                    dve.wait_ge(s_step, 3)
                    dve.reciprocal(weight[:, :], total[:, :]).then_inc(s_step, 1)
                    dve.wait_ge(s_step, 4)
                    dve.tensor_scalar(spreadw[:, :], spreadw[:, :], weight[:, 0:1], None, ALU.mult).then_inc(s_step, 1)
        with ExitStack() as ictx:
            rows = [core.sb(f"rows{i}", [P, GB * S], ctx=ictx) for i in range(2)]
            prod = [core.sb(f"prod{i}", [P, GB * S], ctx=ictx) for i in range(2)]
            s_in = [core.sem(f"{name}_in{i}", ictx) for i in range(2)]
            s_prod, s_hc = (Signal(core, f"{name}_{n}", ictx, 2) for n in ("prod", "hc"))
            with nc.Block() as block:

                @block.sync
                def _(sp):
                    start_ahead(sp, (s_prod, s_hc))

                    def slot(i, j, live):
                        sp.wait_ge(s_prod.sem, s_prod.after(i - 1))
                        src = wide[bass.ds(i * GB, GB), :].rearrange("b s -> (b s)").partition_broadcast(P)
                        sp.dma_start(rows[j][:, :], src).then_inc(s_in[j], 16)
                    skewed(sp, steps, 0, 2, slot)

                @block.gpsimd
                def _(pool):
                    def slot(i, j, live):
                        pool.wait_ge(s_in[j], i * 8 + 16 - 8 * j)
                        pool.wait_ge(s_hc.sem, s_hc.after(i - 1))
                        pool.tensor_tensor(prod[j][:, :], rows[j][:, :], core.xnT[:, bass.ds(i * (GB * S), GB * S)],
                                           ALU.mult).then_inc(s_prod.sem, 1)
                    skewed(pool, steps, 0, 2, slot)

                @block.vector
                def _(dve):
                    def slot(i, j, live):
                        dve.wait_ge(s_prod.sem, s_prod.after(i + 1))
                        dve.tensor_reduce(hc[:, bass.ds(i * GB, GB)],
                                          prod[j][:, :].rearrange("p (b s) -> p b s", b=GB), AX.X,
                                          ALU.add).then_inc(s_hc.sem, 1)
                    skewed(dve, steps, 0, 2, slot)
                    dve.wait_ge(s_hc.sem, s_hc.after(steps))


def layer2_gates(nc, core, inp, gate):
    with ExitStack() as ctx:
        logits = core.sb("logits2", [P, B, E2], ctx=ctx)
        oh = [core.sb(f"oh2{i}", [P, B, E2], ctx=ctx) for i in range(2)]
        w = [core.sb(f"w2{i}", [P, B], ctx=ctx) for i in range(2)]
        project_tokens(nc, core, "r2p", core.xnT, inp["f2_gate"], E2, logits)
        top_two(nc, core, "r2k", logits, E2, oh, w)
        combine_gates(nc, core, "r2g", oh, w, E2, core.tanh_g[:, 6:7], gate)


def dense_experts(nc, core, name, w1_dram, w2_dram, gate):
    GB, CH = 4, F2 // P
    steps = B // GB
    with ExitStack() as ctx:
        w1 = core.sb("w1", [P, E2, F2], ctx=ctx)
        w2 = core.sb("w2", [P, E2, CH, D], ctx=ctx)
        hid = [core.sb(f"hid{i}", [P, CH, GB * S], ctx=ctx) for i in range(2)]
        ps_h = [core.ps(f"ps_h{i}", [P, GB * S], ctx) for i in range(CH)]
        ps_y = [core.ps(f"ps_y{i}", [P, GB * D], ctx) for i in range(2)]
        s_w = core.sem(f"{name}_w", ctx)
        s_h, s_rel, s_y, s_upd = (Signal(core, f"{name}_{n}", ctx, a) for n, a in
                                  (("h", 0), ("rel", 4), ("y", 2), ("upd", 3)))

        def units(eng, slot):
            for e in range(E2):
                slot(e, 0, e, e == 0, False)
            with eng.Fori(1, steps) as it:
                for e in range(E2):
                    slot(it * E2 + e, it, e, False, False)
            slot(steps * E2, steps, 0, False, True)

        with nc.Block() as block:

            @block.sync
            def _(sp):
                start_ahead(sp, (s_rel, s_y, s_upd))
                sp.dma_start(w1[:, :, :], w1_dram).then_inc(s_w, 16)
                sp.dma_start(w2[:, :, :, :], w2_dram).then_inc(s_w, 16)
                sp.wait_ge(s_w, 32)

            @block.tensor
            def _(pe):
                pe.wait_ge(s_w, 32)

                def slot(u, st, e, first, last):
                    for c in range(CH):
                        if not last:
                            pe.wait_ge(s_rel.sem, s_rel.after(u * CH + c - (CH - 1)))
                            pe.matmul(ps_h[c][:, :], w1[:, e, c * P:(c + 1) * P],
                                      core.xnT[:, bass.ds(st * (GB * S), GB * S)], start=True, stop=True
                                      ).then_inc(s_h.sem, 1)
                    if not first:
                        o = (e - 1) % E2
                        j = o % 2
                        pe.wait_ge(s_rel.sem, s_rel.after(u * CH))
                        pe.wait_ge(s_upd.sem, s_upd.after(u - 2))
                        for b in range(GB):
                            for c in range(CH):
                                mm = pe.matmul(ps_y[j][:, b * D:(b + 1) * D], hid[j][:, c, b * S:(b + 1) * S],
                                               w2[:, o, c, :], start=c == 0, stop=c == CH - 1)
                        mm.then_inc(s_y.sem, 1)
                units(pe, slot)

            @block.scalar
            def _(act):
                def slot(u, st, e, first, last):
                    if last:
                        return
                    act.wait_ge(s_y.sem, s_y.after(u - 1))
                    for c in range(CH):
                        act.wait_ge(s_h.sem, u * CH + c + 1)
                        act.activation(hid[e % 2][:, c, :], ps_h[c][:, :], ACT.Relu).then_inc(s_rel.sem, 1)
                units(act, slot)

            @block.vector
            def _(dve):
                def slot(u, st, e, first, last):
                    if first:
                        return
                    o = (e - 1) % E2
                    dve.wait_ge(s_y.sem, s_y.after(u))
                    dve.wait_ge(s_upd.sem, s_upd.after(u - 1))
                    b0 = (st * GB) if e > 0 else (st * GB - GB)
                    for b in range(GB):
                        xb = core.x[:, bass.ds(b0 + b, 1), :]
                        ins = dve.scalar_tensor_tensor(xb, ps_y[o % 2][:, b * D:(b + 1) * D].unsqueeze(1),
                                                       gate[:, bass.ds((b0 + b) * E2 + o, 1)], xb, ALU.mult, ALU.add)
                    ins.then_inc(s_upd.sem, 1)
                units(dve, slot)
                dve.wait_ge(s_upd.sem, s_upd.after(steps * E2))


def feature_mlps(nc, core, name, inp, coef):
    GB, CH = 4, M3 * I3 // P
    steps = B // GB
    with ExitStack() as ctx:
        w_in = core.sb("w_in", [P, CH, P], ctx=ctx)
        w1, b1, b_in, shift = (core.sb(n, [P, CH], ctx=ctx) for n in ("w1", "b1", "b_in", "shift"))
        w2 = core.sb("w2", [P, CH, P], ctx=ctx)
        b2 = core.sb("b2", [P, 1], ctx=ctx)
        w_out = core.sb("w_out", [P, D], ctx=ctx)
        hid = [core.sb(f"hid{i}", [P, GB * S], ctx=ctx) for i in range(4)]
        g = [core.sb(f"g{i}", [P, GB * S], ctx=ctx) for i in range(2)]
        ps_s = [core.ps(f"ps_s{i}", [P, GB * S], ctx) for i in range(4)]
        ps_g = [core.ps(f"ps_g{i}", [P, GB * S], ctx) for i in range(2)]
        ps_o = [core.ps(f"ps_o{i}", [P, GB * D], ctx) for i in range(2)]
        s_w, s_shift = (core.sem(f"{name}_{n}", ctx) for n in ("w", "shift"))
        s_s, s_hid, s_used, s_g, s_gsb, s_out, s_upd = (Signal(core, f"{name}_{n}", ctx, a) for n, a in (
            ("s", 0), ("hid", 4), ("used", 4), ("g", 2), ("gsb", 3), ("out", 3), ("upd", 3)))
        LAG = 2

        with nc.Block() as block:

            @block.sync
            def _(sp):
                start_ahead(sp, (s_hid, s_used, s_g, s_gsb, s_out, s_upd))
                loads = ((w_in[:, :, :], "f3_in"), (w1[:, :], "f3_w1"), (b1[:, :], "f3_b1"), (b_in[:, :], "f3_bin"),
                         (w2[:, :, :], "f3_w2"), (b2[:, :], "f3_b2"), (w_out[:, :], "f3_out"))
                for dst, src in loads:
                    sp.dma_start(dst, inp[src]).then_inc(s_w, 16)
                sp.wait_ge(s_w, 112)

            @block.tensor
            def _(pe):
                pe.wait_ge(s_w, 112)

                def slot(i, j, live):
                    p = j % 2
                    for c in range(CH + LAG):
                        if live(0) and c < CH:
                            pe.wait_ge(s_hid.sem, s_hid.after(i * CH + c - 3))
                            pe.matmul(ps_s[c % 4][:, :], w_in[:, c, :], core.xnT[:, bass.ds(i * (GB * S), GB * S)],
                                      start=True, stop=True).then_inc(s_s.sem, 1)
                        if live(0) and c >= LAG:
                            k = c - LAG
                            pe.wait_ge(s_hid.sem, s_hid.after(i * CH + k + 1))
                            if k == 0:
                                pe.wait_ge(s_gsb.sem, s_gsb.after(i - 1))
                            mm = pe.matmul(ps_g[p][:, :], w2[:, k, :], hid[k % 4][:, :], start=k == 0,
                                           stop=k == CH - 1)
                            mm.then_inc(s_used.sem, 1)
                        if live(1) and c == LAG:
                            pe.wait_ge(s_gsb.sem, s_gsb.after(i))
                            pe.wait_ge(s_upd.sem, s_upd.after(i - 2))
                            for b in range(GB):
                                mm = pe.matmul(ps_o[1 - p][:, b * D:(b + 1) * D], g[1 - p][:, b * S:(b + 1) * S],
                                               w_out[:, :], start=True, stop=True)
                            mm.then_inc(s_out.sem, 1)
                skewed(pe, steps, 1, 2, slot)

            @block.scalar
            def _(act):
                act.wait_ge(s_shift, 2)

                def slot(i, j, live):
                    for c in range(CH):
                        act.wait_ge(s_s.sem, i * CH + c + 1)
                        act.wait_ge(s_used.sem, s_used.after(i * CH + c - 3))
                        act.activation(hid[c % 4][:, :], ps_s[c % 4][:, :], ACT.Relu, bias=shift[:, c:c + 1],
                                       scale=w1[:, c:c + 1]).then_inc(s_hid.sem, 1)
                skewed(act, steps, 0, 2, slot)

            @block.vector
            def _(dve):
                dve.wait_ge(s_w, 112)
                dve.tensor_tensor(shift[:, :], w1[:, :], b_in[:, :], ALU.mult).then_inc(s_shift, 1)
                dve.wait_ge(s_shift, 1)
                dve.tensor_tensor(shift[:, :], shift[:, :], b1[:, :], ALU.add).then_inc(s_shift, 1)

                def slot(i, j, live):
                    p = j % 2
                    if live(1):
                        dve.wait_ge(s_out.sem, s_out.after(i))
                        for b in range(GB):
                            xb = core.x[:, bass.ds(i * GB + (b - GB), 1), :]
                            ins = dve.scalar_tensor_tensor(xb, ps_o[1 - p][:, b * D:(b + 1) * D].unsqueeze(1), coef,
                                                           xb, ALU.mult, ALU.add)
                        ins.then_inc(s_upd.sem, 1)
                    if live(0):
                        dve.wait_ge(s_used.sem, s_used.after(i * CH + CH))
                        dve.wait_ge(s_out.sem, s_out.after(i - 1))
                        dve.tensor_scalar(g[p][:, :], ps_g[p][:, :], b2[:, 0:1], None, ALU.add).then_inc(s_gsb.sem, 1)
                skewed(dve, steps, 1, 2, slot)
                dve.wait_ge(s_upd.sem, s_upd.after(steps))


def dispatch_tables(nc, core, inp, place, fetch, weight):
    with ExitStack() as ctx:
        oh = [core.sb(f"oh1{i}", [P, B, E1], ctx=ctx) for i in range(2)]
        rank = [core.sb(f"rank{i}", [P, B], ctx=ctx) for i in range(2)]
        w = [core.sb(f"w1{i}", [P, B], ctx=ctx) for i in range(2)]
        with ExitStack() as lctx:
            logits = core.sb("logits1", [P, B, E1], ctx=lctx)
            project_tokens(nc, core, "r1p", core.xnT, inp["f1_gate"], E1, logits, inp["f1_gate_b"])
            top_two(nc, core, "r1k", logits, E1, oh, w, rank)
        chosen = core.sb("chosen", [P, B * E1], ctx=ctx)
        ahead = core.sb("ahead", [P, B * E1], ctx=ctx)
        counts = [core.sb(f"counts{i}", [P, B * E1], ctx=ctx) for i in range(2)]
        before = core.sb("before", [P, P], ctx=ctx)
        ones = core.sb("ones", [P, P], ctx=ctx)
        pos, full, row, base = (core.sb(n, [P, B], ctx=ctx) for n in ("pos", "full", "row", "base"))
        N, BANKS = B * E1, B * E1 // 512
        ps_b = [core.ps(f"ps_b{i}", [P, 512], ctx) for i in range(BANKS)]
        ps_n = [core.ps(f"ps_n{i}", [P, 512], ctx) for i in range(BANKS)]
        s_c, s_step, s_mm = (core.sem(f"r1t_{n}", ctx) for n in ("c", "step", "mm"))
        with nc.Block() as block:

            @block.sync
            def _(sp):
                sp.dma_start(before[:, :], inp["before"]).then_inc(s_c, 16)
                sp.wait_ge(s_c, 17)

            @block.gpsimd
            def _(pool):
                pool.memset(ones[:, :], 1.0).then_inc(s_c, 1)

            @block.tensor
            def _(pe):
                pe.wait_ge(s_c, 17)
                pe.wait_ge(s_step, 1)
                for i in range(BANKS):
                    cols = slice(i * 512, (i + 1) * 512)
                    pe.matmul(ps_b[i][:, :], before[:, :], chosen[:, cols], start=True, stop=True).then_inc(s_mm, 1)
                    pe.matmul(ps_n[i][:, :], ones[:, :], chosen[:, cols], start=True, stop=True).then_inc(s_mm, 1)

            @block.vector
            def _(dve):
                done = [0]

                def step(ins):
                    done[0] += 1
                    ins.then_inc(s_step, 1)
                    dve.wait_ge(s_step, done[0])

                def flat(t):
                    return t[:, :, :].rearrange("p b e -> p (b e)")

                step(dve.tensor_tensor(chosen[:, :], flat(oh[0]), flat(oh[1]), ALU.add))
                dve.wait_ge(s_mm, 2 * BANKS)
                for i in range(BANKS):
                    cols = slice(i * 512, (i + 1) * 512)
                    step(dve.tensor_copy(ahead[:, cols], ps_b[i][:, :]))
                    step(dve.tensor_copy(counts[0][:, cols], ps_n[i][:, :]))
                src, shift = 0, E1
                while shift < N:
                    a, z = counts[src], counts[1 - src]
                    step(dve.tensor_copy(z[:, 0:shift], a[:, 0:shift]))
                    step(dve.tensor_tensor(z[:, shift:N], a[:, shift:N], a[:, 0:N - shift], ALU.add))
                    src, shift = 1 - src, shift * 2
                step(dve.tensor_tensor(ahead[:, E1:N], ahead[:, E1:N], counts[src][:, 0:N - E1], ALU.add))
                for i in range(2):
                    o = flat(oh[i])
                    step(dve.tensor_tensor(o, o, ahead[:, :], ALU.mult))
                    step(dve.tensor_reduce(pos[:, :], oh[i][:, :, :], AX.X, ALU.add))
                    step(dve.tensor_scalar(full[:, :], pos[:, :], float(CAP), None, ALU.is_ge))
                    step(dve.tensor_scalar(base[:, :], rank[i][:, :], -float(ROWS1), float(E1 * ROWS1), ALU.mult,
                                           ALU.add))
                    step(dve.tensor_tensor(row[:, :], base[:, :], pos[:, :], ALU.add))
                    step(dve.scalar_tensor_tensor(row[:, :], full[:, :], float(2 ** 20), row[:, :], ALU.mult, ALU.add))
                    step(dve.tensor_copy(place[:, :, i], row[:, :]))
                    step(dve.tensor_scalar(pos[:, :], pos[:, :], float(CAP - 1), None, ALU.min))
                    step(dve.tensor_tensor(row[:, :], base[:, :], pos[:, :], ALU.add))
                    step(dve.tensor_copy(fetch[:, :, i], row[:, :]))
                    step(dve.tensor_scalar(full[:, :], full[:, :], -1.0, 1.0, ALU.mult, ALU.add))
                    step(dve.scalar_tensor_tensor(weight[i][:, :], w[i][:, :], core.tanh_g[:, 5:6], full[:, :],
                                                  ALU.mult, ALU.mult))


FILL = 8


def clear_rows(nc, core, xe, zero, s_fill):
    with nc.Block() as block:

        @block.vector
        def _(dve):
            dve.memset(zero[:, :], 0.0).then_inc(s_fill[0], 1)

        @block.sync
        def _(sp):
            sp.wait_ge(s_fill[0], 1)
            rows = xe.rearrange("(f p r) d -> f p (r d)", f=FILL, p=P)
            for f in range(FILL):
                sp.dma_start(rows[f], zero[:, :]).then_inc(s_fill[1], 16)


def scatter_tokens(nc, core, xe, place, s_fill):
    GB = 4
    steps = B // GB
    with ExitStack() as ctx:
        xn = [[core.sb(f"sc_xn{i}{b}", [P, D], ctx=ctx) for b in range(GB)] for i in range(2)]
        idx = [[[core.sb(f"sc_idx{i}{b}{k}", [P, 1], U32, ctx=ctx) for k in range(2)] for b in range(GB)]
               for i in range(2)]
        s_sent = [core.sem(f"sc_sent{i}", ctx) for i in range(2)]
        s_xn, s_idx, s_go = (core.sem(f"sc_{n}", ctx) for n in ("xn", "idx", "go"))
        with nc.Block() as block:

            @block.vector
            def _(dve):
                def slot(i, j, used):
                    if used:
                        dve.wait_ge(s_sent[j], (i - j) * (GB * 16))
                    for b in range(GB):
                        bb = i * GB + b
                        for k in range(2):
                            dve.tensor_copy(idx[j][b][k][:, :], place[:, bass.ds(bb, 1), k]).then_inc(s_idx, 1)
                        dve.tensor_scalar(xn[j][b][:, :], core.x[:, bass.ds(bb, 1), :].rearrange("p a d -> p (a d)"),
                                          core.mean[:, bass.ds(bb, 1)], core.rstd[:, bass.ds(bb, 1)], ALU.subtract,
                                          ALU.mult).then_inc(s_xn, 1)
                for i in range(2):
                    slot(i, i, False)
                with dve.Fori(1, steps // 2) as it:
                    for j in range(2):
                        slot(it * 2 + j, j, True)

            @block.gpsimd
            def _(pool):
                pool.wait_ge(s_fill[1], 16 * FILL)

                def slot(i, j, live):
                    pool.wait_ge(s_xn, i * GB + GB)
                    pool.wait_ge(s_idx, i * (2 * GB) + 2 * GB)
                    pool.sem_inc(s_go, 1)
                    for b in range(GB):
                        for k in range(2):
                            pool.indirect_dma_start(xe, bass.IndirectOffsetOnAxis(idx[j][b][k][:, :], 0),
                                                    xn[j][b][:, :], None, bounds_check=E1 * ROWS1 - 1,
                                                    oob_is_err=False).then_inc(s_sent[j], 16)
                skewed(pool, steps, 0, 2, slot)
                for s in s_sent:
                    pool.wait_ge(s, steps // 2 * GB * 2 * 16)


def expert_mlps(nc, core, name, inp, xe, ye):
    CH, FC, HALF = ROWS1 // P, F1 // P, ROWS1 // 2
    with ExitStack() as ctx:
        rows = [core.sb(f"rows{i}", [P, CH, D], ctx=ctx) for i in range(2)]
        rowsT = [core.sb(f"rowsT{i}", [P, ROWS1], ctx=ctx) for i in range(2)]
        w1 = [core.sb(f"e_w1{i}", [P, F1], ctx=ctx) for i in range(4)]
        w2 = [core.sb(f"e_w2{i}", [P, FC, D], ctx=ctx) for i in range(4)]
        b1 = [core.sb(f"e_b1{i}", [P, FC], ctx=ctx) for i in range(4)]
        b2 = [core.sb(f"e_b2{i}", [P, D], ctx=ctx) for i in range(4)]
        hid = [core.sb(f"e_hid{i}", [P, FC, ROWS1], ctx=ctx) for i in range(2)]
        out = [core.sb(f"e_out{i}", [P, CH, D], ctx=ctx) for i in range(2)]
        ps_x = [core.ps(f"ps_x{i}", [P, 512], ctx) for i in range(2)]
        ps_h = [core.ps(f"ps_h{i}", [P, 512], ctx) for i in range(4)]
        ps_y = [core.ps(f"ps_y{i}", [P, 512], ctx) for i in range(2)]
        s_w = [core.sem(f"{name}_w{i}", ctx) for i in range(4)]
        s_in = [core.sem(f"{name}_in{i}", ctx) for i in range(2)]
        s_st = [core.sem(f"{name}_st{i}", ctx) for i in range(2)]
        s_tr, s_xT, s_h, s_gelu, s_y, s_out = (Signal(core, f"{name}_{n}", ctx, a) for n, a in (
            ("tr", 2), ("xT", 2), ("h", 8), ("gelu", 8), ("y", 4), ("out", 3)))

        def chunks(t, lo, hi):
            return t[:, 0:(hi - lo) * D].rearrange("p (c d) -> p c d", c=hi - lo)

        with nc.Block() as block:

            @block.sync
            def _(sp):
                start_ahead(sp, (s_tr, s_xT, s_h, s_gelu, s_y, s_out))
                for s in s_st:
                    sp.sem_inc(s, 16)

                def slot(i, j, live):
                    p = j % 2
                    if live(0):
                        sp.wait_ge(s_tr.sem, s_tr.after(i - 1))
                        sp.dma_start(rows[p][:, :, :], xe[bass.ds(i * ROWS1, ROWS1), :]
                                     .rearrange("(c p) d -> p c d", p=P)).then_inc(s_in[p], 16)
                        sp.wait_ge(s_y.sem, s_y.after(i - 3))
                        e = bass.ds(i, 1)
                        sp.dma_start(w1[j][:, :], inp["f1_w1"][e, :, :].rearrange("a d f -> (a d) f")
                                     ).then_inc(s_w[j], 16)
                        sp.dma_start(b1[j][:, :], inp["f1_b1"][e, :, :].rearrange("a p c -> (a p) c")
                                     ).then_inc(s_w[j], 16)
                        sp.dma_start(w2[j][:, :, :], inp["f1_w2"][e, :, :].rearrange("a (c p) d -> p (a c) d", p=P)
                                     ).then_inc(s_w[j], 16)
                        sp.dma_start(b2[j][:, :], inp["f1_b2"][e, :].rearrange("a d -> (a d)").partition_broadcast(P)
                                     ).then_inc(s_w[j], 16)
                    if live(3):
                        sp.wait_ge(s_out.sem, s_out.after(i - 2))
                        sp.dma_start(ye[bass.ds(i * ROWS1 - 3 * ROWS1, ROWS1), :].rearrange("(c p) d -> p c d", p=P),
                                     out[1 - p][:, :, :]).then_inc(s_st[1 - p], 16)
                skewed(sp, E1, 3, 4, slot)
                for s in s_st:
                    sp.wait_ge(s, (E1 // 2 + 1) * 16)

            @block.tensor
            def _(pe):
                def slot(i, j, live):
                    p = j % 2
                    if live(0):
                        pe.wait_ge(s_in[p], (i - p) * 8 + 16)
                        pe.wait_ge(s_xT.sem, s_xT.after(i))
                        for c in range(CH):
                            mm = pe.transpose(ps_x[c // 4][:, c % 4 * P:(c % 4 + 1) * P], rows[p][:, c, :],
                                              core.ident[:, :])
                        mm.then_inc(s_tr.sem, 1)
                    if live(2):
                        pe.wait_ge(s_gelu.sem, s_gelu.after(i * 8 - 8))
                        pe.wait_ge(s_out.sem, s_out.after(i - 2))
                        for c in range(CH):
                            for f in range(FC):
                                mm = pe.matmul(ps_y[c // 4][:, c % 4 * D:(c % 4 + 1) * D],
                                               hid[p][:, f, c * P:(c + 1) * P], w2[(j - 2) % 4][:, f, :],
                                               start=f == 0, stop=f == FC - 1)
                        mm.then_inc(s_y.sem, 1)
                    if live(1):
                        pe.wait_ge(s_w[(j - 1) % 4], (i - 1 - (j - 1) % 4) * 16 + 64)
                        pe.wait_ge(s_xT.sem, s_xT.after(i))
                        for f in range(FC):
                            for h in range(2):
                                n = 2 * f + h
                                pe.wait_ge(s_gelu.sem, s_gelu.after(i * 8 - 8 + n - 3))
                                pe.matmul(ps_h[n % 4][:, 0:HALF], w1[(j - 1) % 4][:, f * P:(f + 1) * P],
                                          rowsT[1 - p][:, h * HALF:(h + 1) * HALF], start=True, stop=True
                                          ).then_inc(s_h.sem, 1)
                skewed(pe, E1, 2, 4, slot)

            @block.scalar
            def _(act):
                def slot(i, j, live):
                    p = j % 2
                    if live(1):
                        act.wait_ge(s_w[(j - 1) % 4], (i - 1 - (j - 1) % 4) * 16 + 64)
                        act.wait_ge(s_y.sem, s_y.after(i - 2))
                        for f in range(FC):
                            for h in range(2):
                                n = 2 * f + h
                                act.wait_ge(s_h.sem, s_h.after(i * 8 - 8 + n + 1))
                                act.activation(hid[1 - p][:, f, h * HALF:(h + 1) * HALF], ps_h[n % 4][:, 0:HALF],
                                               ACT.Gelu, bias=b1[(j - 1) % 4][:, f:f + 1]).then_inc(s_gelu.sem, 1)
                skewed(act, E1, 1, 4, slot)

            @block.vector
            def _(dve):
                def slot(i, j, live):
                    p = j % 2
                    if live(0):
                        dve.wait_ge(s_tr.sem, s_tr.after(i + 1))
                        dve.wait_ge(s_h.sem, s_h.after(i * 8 - 8))
                        dve.tensor_copy(rowsT[p][:, 0:512], ps_x[0][:, :])
                        dve.tensor_copy(rowsT[p][:, 512:ROWS1], ps_x[1][:, 0:ROWS1 - 512]).then_inc(s_xT.sem, 1)
                    if live(2):
                        dve.wait_ge(s_w[(j - 2) % 4], (i - 2 - (j - 2) % 4) * 16 + 64)
                        dve.wait_ge(s_y.sem, s_y.after(i - 1))
                        dve.wait_ge(s_st[p], (i - 2 - p) * 8 + 16)
                        for lo, hi in ((0, 4), (4, CH)):
                            ins = dve.tensor_tensor(out[p][:, lo:hi, :], chunks(ps_y[lo // 4], lo, hi),
                                                    b2[(j - 2) % 4][:, :].unsqueeze(1).to_broadcast([P, hi - lo, D]),
                                                    ALU.add)
                        ins.then_inc(s_out.sem, 1)
                skewed(dve, E1, 2, 4, slot)


def gather_outputs(nc, core, ye, fetch, weight):
    GB = 4
    steps = B // GB
    with ExitStack() as ctx:
        y = [[[core.sb(f"ga_y{i}{b}{k}", [P, D], ctx=ctx) for k in range(2)] for b in range(GB)] for i in range(2)]
        idx = [[[core.sb(f"ga_idx{i}{b}{k}", [P, 1], U32, ctx=ctx) for k in range(2)] for b in range(GB)]
               for i in range(2)]
        s_got = [core.sem(f"ga_got{i}", ctx) for i in range(2)]
        s_idx, s_first, s_go = (core.sem(f"ga_{n}", ctx) for n in ("idx", "first", "go"))
        s_upd = Signal(core, "ga_upd", ctx, 3)
        with nc.Block() as block:

            @block.sync
            def _(sp):
                start_ahead(sp, (s_upd,))

            @block.gpsimd
            def _(pool):
                def slot(i, j, live):
                    pool.wait_ge(s_idx, i + 1)
                    pool.wait_ge(s_upd.sem, s_upd.after(i - 1))
                    pool.sem_inc(s_go, 1)
                    for b in range(GB):
                        for k in range(2):
                            pool.indirect_dma_start(y[j][b][k][:, :], None, ye,
                                                    bass.IndirectOffsetOnAxis(idx[j][b][k][:, :], 0)
                                                    ).then_inc(s_got[j], 16)
                skewed(pool, steps, 0, 2, slot)

            @block.vector
            def _(dve):
                def slot(i, j, live):
                    if live(0):
                        if not isinstance(i, int) or i >= 2:
                            dve.wait_ge(s_got[j], (i - j) * (GB * 16))
                        for b in range(GB):
                            for k in range(2):
                                ins = dve.tensor_copy(idx[j][b][k][:, :], fetch[:, bass.ds(i * GB + b, 1), k])
                        ins.then_inc(s_idx, 1)
                    if live(1):
                        dve.wait_ge(s_got[1 - j], (i - 1 - (1 - j)) * (GB * 16) + GB * 2 * 16)
                        for k in range(2):
                            if k == 1:
                                dve.wait_ge(s_first, i)
                            for b in range(GB):
                                bb = i * GB + (b - GB)
                                xb = core.x[:, bass.ds(bb, 1), :]
                                ins = dve.scalar_tensor_tensor(xb, y[1 - j][b][k][:, :].unsqueeze(1),
                                                               weight[k][:, bass.ds(bb, 1)], xb, ALU.mult, ALU.add)
                            ins.then_inc(s_first if k == 0 else s_upd.sem, 1)
                skewed(dve, steps, 1, 2, slot)
                dve.wait_ge(s_upd.sem, s_upd.after(steps))


def routed_experts(nc, core, inp):
    xe = nc.dram_tensor("f1_xe", (E1 * ROWS1, D), F32, kind="Internal").ap()
    ye = nc.dram_tensor("f1_ye", (E1 * ROWS1, D), F32, kind="Internal").ap()
    with ExitStack() as ctx:
        place = core.sb("place", [P, B, 2], U32, ctx)
        fetch = core.sb("fetch", [P, B, 2], U32, ctx)
        weight = [core.sb(f"weight{i}", [P, B], ctx=ctx) for i in range(2)]
        with ExitStack() as fctx:
            zero = core.sb("zero_rows", [P, E1 * ROWS1 * D // P // FILL], ctx=fctx)
            s_fill = [core.sem(f"f1_fill{i}", fctx) for i in range(2)]
            clear_rows(nc, core, xe, zero, s_fill)
            dispatch_tables(nc, core, inp, place, fetch, weight)
            scatter_tokens(nc, core, xe, place, s_fill)
        expert_mlps(nc, core, "f1", inp, xe, ye)
        gather_outputs(nc, core, ye, fetch, weight)


def program(nc, inp, out, stages):
    with ExitStack() as ctx:
        core = Core(nc, ctx)
        core.inp = inp
        load_inputs(nc, core, inp)
        g = core.tanh_g
        if "x0" in stages:
            layernorm_transpose(nc, core, "ln0")
            head_attention(nc, core, "x0", inp["x0_wq"], inp["x0_wk"], inp["x0_wv"], inp["x0_wo"],
                           scale=float(D) ** -0.5, mask=inp["mask"], coef=g[:, 0:1])
        if "f0" in stages:
            layernorm_transpose(nc, core, "ln1")
            with ExitStack() as fctx:
                gate = core.sb("gate0", [P, B * E0], ctx=fctx)
                layer0_gates(nc, core, inp, gate)
                head_attention(nc, core, "f0", inp["f0_wq"], inp["f0_wk"], inp["f0_wv"], inp["f0_wo"],
                               scale=float(HD) ** -0.5, bias=(inp["f0_bq"], inp["f0_bk"], inp["f0_bv"]),
                               ctx_keys=False, experts=E0, gate=gate)
        core.recycle_semaphores()
        if "x1" in stages:
            layernorm_transpose(nc, core, "ln2")
            context_attention(nc, core, "x1", inp["x1_wo"], float(HD) ** -0.5, g[:, 1:2])
        if "f1" in stages:
            layernorm_transpose(nc, core, "ln3")
            routed_experts(nc, core, inp)
        core.recycle_semaphores()
        if "x2" in stages:
            layernorm_transpose(nc, core, "ln4")
            head_attention(nc, core, "x2", inp["x2_wq"], inp["x2_wk"], inp["x2_wv"], inp["x2_wo"],
                           scale=float(HD) ** -0.5, coef=g[:, 2:3], sigmoid=True)
        if "f2" in stages:
            layernorm_transpose(nc, core, "ln5")
            with ExitStack() as fctx:
                gate = core.sb("gate2", [P, B * E2], ctx=fctx)
                layer2_gates(nc, core, inp, gate)
                dense_experts(nc, core, "f2", inp["f2_w1"], inp["f2_w2"], gate)
        core.recycle_semaphores()
        if "x3" in stages:
            layernorm_transpose(nc, core, "ln6")
            with ExitStack() as fctx:
                hc = core.sb("hc", [P, B], ctx=fctx)
                best_token_context(nc, core, "x3b", inp["x3_w_sim"], inp["x3_w1"], inp["x3_b_sim"], hc)
                context_attention(nc, core, "x3", None, 1.0, g[:, 3:4],
                                  mix=(inp["x3_w_sim"], inp["x3_w4"], hc, inp["x3_b"]))
        if "f3" in stages:
            layernorm_transpose(nc, core, "ln7")
            feature_mlps(nc, core, "f3", inp, g[:, 7:8])
        store_output(nc, core, out)


def block_diagonal_heads(np, w):
    z = np.zeros((1, D, D), w.dtype)
    for h in range(HEADS):
        z[0, HD * h:HD * h + HD, HD * h:HD * h + HD] = w.T
    return z


def output_rows(np, wo, bo=None):
    z = np.zeros((wo.shape[0], 2, P, D), wo.dtype)
    for t in range(SETS):
        for s in range(4):
            h = 4 * t + s
            half, row = (0, 32 * s + HD * t) if t < 3 else (1, 32 * s + 24)
            z[:, half, row:row + HD, :] = wo[:, :, HD * h:HD * h + HD].transpose(0, 2, 1)
    if bo is not None:
        z[:, 1, 0, :] = bo
    return z


def sum_row(t, s):
    return 32 * s + 24 + t


def spread_rows(np):
    z = np.zeros((P, 2, P), np.float32)
    for s in range(4):
        for r in range(32):
            t = r // HD if r < 24 else r - 24
            if r < 28:
                z[sum_row(t, s), 0, 32 * s + r] = 1.0
            z[sum_row(3, s), 1, 32 * s + r] = 1.0
    return z


def sum_rows(np):
    z = np.zeros((P, 2), np.float32)
    z[:, 1] = 1.0
    for s in range(4):
        for t in range(SETS):
            z[sum_row(t, s)] = 1.0, 0.0
    return z


def dim_head_set(np, w):
    v = w.reshape(w.shape[:-1] + (SETS, 4, HD))
    n = v.ndim
    return np.ascontiguousarray(v.transpose(tuple(range(n - 3)) + (n - 1, n - 2, n - 3)).reshape(w.shape))


def row_padded(np, v):
    z = np.zeros((v.shape[0], P, 2), v.dtype)
    for t in range(SETS):
        for s in range(4):
            h = 4 * t + s
            half, row = (0, 32 * s + HD * t) if t < 3 else (1, 32 * s + 24)
            z[:, row:row + HD, half] = v[:, HD * h:HD * h + HD]
    return z


def padded(np, v, shape):
    z = np.zeros(shape, v.dtype)
    z[tuple(slice(0, n) for n in v.shape)] = v
    return z


def chunked(np, v):
    return np.ascontiguousarray(v.reshape(-1, P).T)


def grouped(np, w):
    z = np.zeros((M3 * I3, P), w.dtype)
    for m in range(M3):
        z[I3 * m:I3 * m + I3, m] = w[m]
    return np.ascontiguousarray(z.reshape(-1, P, P).transpose(1, 0, 2))


def feature_bias(np, b):
    z = np.zeros((P, 1), b.dtype)
    z[:M3, 0] = b
    z[M3, 0] = 1.0
    return z


def laid_out(np, a):
    def c(v):
        return np.ascontiguousarray(v)

    return {
        "x": c(a["x"]), "ctx_1024": c(a["ctx_1024"]), "mask": c(a["mask_1x1xSxS2_ik1"].reshape(S, NC)),
        "g_xattn": c(a["g_xattn"]), "g_ffn": c(a["g_ffn"]), "spread": spread_rows(np), "is_sum": sum_rows(np),
        "x0_wq": dim_head_set(np, block_diagonal_heads(np, a["L0_xattn_Wq"])), "x0_wk": dim_head_set(np, block_diagonal_heads(np, a["L0_xattn_Wk"])),
        "x0_wv": block_diagonal_heads(np, a["L0_xattn_Wv"]),
        "x0_wo": output_rows(np, a["L0_xattn_Wo"][None], a["L0_xattn_bo"][None]),
        "r0_w1": padded(np, a["L0_ffn_rW1"].T, (P, P)), "r0_b1": padded(np, a["L0_ffn_rb1"][:, None], (P, 1)),
        "ln_g": c(a["L0_ffn_ln_g"]), "ln_b": c(a["L0_ffn_ln_b"]),
        "r0_w2": padded(np, a["L0_ffn_rW2"].T, (P, P)), "r0_b2": padded(np, a["L0_ffn_rb2"][:, None], (P, 1)),
        "f0_wq": dim_head_set(np, a["L0_ffn_qW"].transpose(0, 2, 1)), "f0_bq": dim_head_set(np, a["L0_ffn_qb"]),
        "f0_wk": dim_head_set(np, a["L0_ffn_kW"].transpose(0, 2, 1)), "f0_bk": dim_head_set(np, a["L0_ffn_kb"]),
        "f0_wv": c(a["L0_ffn_vW"].transpose(0, 2, 1)), "f0_bv": row_padded(np, a["L0_ffn_vb"]),
        "f0_wo": output_rows(np, a["L0_ffn_oW"], a["L0_ffn_ob"]),
        "x1_wo": c(a["L1_xattn_W_out"].T),
        "f1_gate": padded(np, a["L1_ffn_gate_w"], (P, P)), "f1_gate_b": padded(np, a["L1_ffn_gate_b"][:, None], (P, 1)),
        "f1_w1": c(a["L1_ffn_w1"]), "f1_b1": c(a["L1_ffn_b1"].reshape(E1, F1 // P, P).transpose(0, 2, 1)),
        "f1_w2": c(a["L1_ffn_w2"]), "f1_b2": c(a["L1_ffn_b2"]),
        "before": np.triu(np.ones((P, P), np.float32), 1),
        "f2_gate": padded(np, a["L2_ffn_gate_w"], (P, P)), "f2_w1": c(a["L2_ffn_w1"].transpose(1, 0, 2)),
        "f2_w2": c(a["L2_ffn_w2"].reshape(E2, F2 // P, P, D).transpose(2, 0, 1, 3)),
        "x3_w_sim": c(np.stack([a["L3_xattn_w_sim"][2 * D:], a["L3_xattn_w_sim"][D:2 * D]], axis=1)),
        "x3_w1": padded(np, a["L3_xattn_w_sim"][:D, None], (P, P)), "x3_b_sim": padded(np, a["L3_xattn_b_sim"][:, None], (P, 1)),
        "x3_w4": c(a["L3_xattn_W_qv"].reshape(4, D, D).transpose(1, 0, 2)), "x3_b": c(a["L3_xattn_b_qv"]),
        "f3_in": c(np.repeat(a["L3_ffn_Win"], I3, axis=1).reshape(D, M3 * I3 // P, P)),
        "f3_w1": chunked(np, a["L3_ffn_W1"].reshape(-1)), "f3_b1": chunked(np, a["L3_ffn_b1"].reshape(-1)),
        "f3_bin": chunked(np, np.repeat(a["L3_ffn_bin_"], I3)), "f3_w2": grouped(np, a["L3_ffn_W2"]),
        "f3_b2": feature_bias(np, a["L3_ffn_b2"]),
        "f3_out": padded(np, np.concatenate([a["L3_ffn_Wout"], a["L3_ffn_bout"][None]]), (P, D)),
        "x2_wq": dim_head_set(np, a["L2_xattn_Wq"].T[None]), "x2_wk": dim_head_set(np, a["L2_xattn_Wk"].T[None]),
        "x2_wv": c(a["L2_xattn_Wv"].T[None]), "x2_wo": output_rows(np, a["L2_xattn_Wo"][None]),
    }


def kernel(**inputs):
    import numpy as _np
    import concourse.bacc as _bacc
    from concourse import mybir as _mybir
    from concourse.bass_utils import run_bass_kernel_spmd as _run

    nc = _bacc.Bacc("TRN2", target_bir_lowering=False, num_devices=1)
    arrays, args = {}, {}
    for name, a in laid_out(_np, {k: _np.asarray(v) for k, v in inputs.items()}).items():
        arrays[f"in_{name}_dram"] = a
        args[name] = nc.dram_tensor(f"in_{name}_dram", a.shape, _mybir.dt.from_np(a.dtype), kind="ExternalInput").ap()
    out = nc.dram_tensor("out_dram", (B, S, D), _mybir.dt.from_np(_np.dtype("float32")), kind="ExternalOutput").ap()
    program(nc, args, out, STAGES)
    r = _run(nc, [arrays], core_ids=[0])
    return r.results[0]["out_dram"]
```
